# Optimizing a Trainium2 kernel written in Bass

```python
import numpy as np
import jax
import jax.numpy as jnp

def _softmax(x, axis=-1):
    return jax.nn.softmax(x, axis=axis)

def _gelu(x):
    return jax.nn.gelu(x, approximate=True)

def _silu(x):
    return jax.nn.silu(x)

def _sigmoid(x):
    return jax.nn.sigmoid(x)

def _layernorm(x, axis=-1, eps=1e-05):
    m = jnp.mean(x, axis=axis, keepdims=True)
    v = jnp.var(x, axis=axis, keepdims=True)
    return (x - m) / jnp.sqrt(v + eps)

def _scatter_add(tgt, idx, src, axis=0):
    return tgt.at[idx].add(src)

def _segment_sum(src, seg, n):
    return jax.ops.segment_sum(src, seg, n)
kernel_name = 'mk_prb_d1_jaxref_r8_cae25f'

def setup_inputs(seed: int=0):
    np.random.seed(seed)
    _w = jnp.asarray

    def _L0_attn_setup():
        import jax, jax.numpy as jnp
        import numpy as np
        D_MODEL = 128
        N_HEADS = 16
        D_LATENT = 32
        HEAD_DIM = D_MODEL // N_HEADS

        def apply_rope(x):
            B, T, H, D = x.shape
            inv_freq = 1.0 / 10000.0 ** (jnp.arange(0, D, 2, dtype=jnp.float32) / D)
            t = jnp.arange(T, dtype=jnp.float32)
            freqs = t[:, None] * inv_freq[None, :]
            sin_f = jnp.sin(freqs)[None, :, None, :]
            cos_f = jnp.cos(freqs)[None, :, None, :]
            x1, x2 = jnp.split(x, 2, axis=-1)
            return jnp.concatenate([x1 * cos_f - x2 * sin_f, x1 * sin_f + x2 * cos_f], axis=-1)
        key = jax.random.key(seed)
        ks = jax.random.split(key, 10)
        B, T = (4, 512)
        s = lambda fan_in: 1.0 / np.sqrt(fan_in)
        return {'x': jax.random.normal(ks[0], (B, T, D_MODEL), dtype=jnp.float32), 'Wq': jax.random.normal(ks[1], (D_MODEL, D_MODEL), dtype=jnp.float32) * s(D_MODEL), 'bq': jnp.zeros((D_MODEL,), jnp.float32), 'Wdown': jax.random.normal(ks[2], (D_MODEL, D_LATENT), dtype=jnp.float32) * s(D_MODEL), 'bdown': jnp.zeros((D_LATENT,), jnp.float32), 'Wup': jax.random.normal(ks[3], (D_LATENT, 2 * D_MODEL), dtype=jnp.float32) * s(D_LATENT), 'bup': jnp.zeros((2 * D_MODEL,), jnp.float32), 'Wout': jax.random.normal(ks[4], (D_MODEL, D_MODEL), dtype=jnp.float32) * s(D_MODEL), 'bout': jnp.zeros((D_MODEL,), jnp.float32)}
    _L0_attn_in = _L0_attn_setup()

    def _L0_ffn_setup():
        import jax, jax.numpy as jnp
        import numpy as np
        DIM = 128
        DEPTH = 6
        HEADS = 16
        DIM_HEAD = 64
        WINDOW = 32
        INNER = HEADS * DIM_HEAD
        DIM_INNER = int(DIM * 4 * 2 / 3)
        QK_SCALE = 8.0

        def shift_tokens(t):
            a, s = jnp.split(t, 2, -1)
            s = jnp.pad(s, ((0, 0), (1, 0), (0, 0)))[:, :-1]
            return jnp.concatenate([a, s], -1)

        def l2norm(t):
            return t / jnp.maximum(jnp.linalg.norm(t, axis=-1, keepdims=True), 1e-12)

        def rotate_half(x):
            x1, x2 = jnp.split(x, 2, -1)
            return jnp.concatenate([-x2, x1], -1)

        def rotary_tables(n):
            half = jnp.arange(0, DIM_HEAD, 2, dtype=jnp.float32)
            inv_freq = 1.0 / 10000.0 ** (half / DIM_HEAD)
            t = jnp.arange(n, dtype=jnp.float32)
            freqs = t[:, None] * inv_freq[None, :]
            freqs = jnp.concatenate([freqs, freqs], -1)
            base_scale = (half + 0.4 * DIM_HEAD) / (1.4 * DIM_HEAD)
            power = (t - n // 2) / (WINDOW // 2)
            scale = base_scale[None, :] ** power[:, None]
            scale = jnp.concatenate([scale, scale], -1)
            return (freqs, scale)

        def local_attention(q, k, v):
            b, h, n, d = q.shape
            w = WINDOW
            nw = n // w
            bq = q.reshape(b, h, nw, w, d)
            bk = k.reshape(b, h, nw, w, d)
            bv = v.reshape(b, h, nw, w, d)

            def look(t):
                p = jnp.pad(t, ((0, 0), (0, 0), (1, 0), (0, 0), (0, 0)))
                return jnp.concatenate([p[:, :, :nw], p[:, :, 1:]], axis=3)
            bk2, bv2 = (look(bk), look(bv))
            seq = jnp.arange(n).reshape(nw, w)
            seq_p = jnp.pad(seq, ((1, 0), (0, 0)), constant_values=-1)
            jt = jnp.concatenate([seq_p[:nw], seq_p[1:]], axis=1)
            it = seq[:, :, None]
            jb = jt[:, None, :]
            mask = (it < jb) | (it > jb + w) | (jb == -1)
            sim = jnp.einsum('bhwie,bhwje->bhwij', bq, bk2) * QK_SCALE
            sim = jnp.where(mask, -jnp.finfo(sim.dtype).max, sim)
            attn = jax.nn.softmax(sim, -1)
            out = jnp.einsum('bhwij,bhwje->bhwie', attn, bv2)
            return out.reshape(b, h, n, d)

        def attn_layer(x, Wqkv, qs, ksc, Wo):
            b, n, _ = x.shape
            qkv = x @ Wqkv
            q, k, v = jnp.split(qkv, 3, -1)
            sh = lambda t: t.reshape(b, n, HEADS, DIM_HEAD).transpose(0, 2, 1, 3)
            q, k, v = (sh(q), sh(k), sh(v))
            q = l2norm(q) * qs
            k = l2norm(k) * ksc
            freqs, scale = rotary_tables(n)
            cos, sin = (jnp.cos(freqs), jnp.sin(freqs))
            q = q * cos * scale + rotate_half(q) * sin * scale
            inv = 1.0 / scale
            k = k * cos * inv + rotate_half(k) * sin * inv
            out = local_attention(q, k, v)
            out = out.transpose(0, 2, 1, 3).reshape(b, n, INNER)
            return out @ Wo

        def ffn_layer(x, g, bln, W1, b1, W2, b2):
            mu = x.mean(-1, keepdims=True)
            var = ((x - mu) ** 2).mean(-1, keepdims=True)
            xn = (x - mu) / jnp.sqrt(var + 1e-05) * g + bln
            hg = xn @ W1 + b1
            a, gate = jnp.split(hg, 2, -1)
            return a * jax.nn.gelu(gate, approximate=False) @ W2 + b2
        key = jax.random.key(seed)
        ks = jax.random.split(key, 8)
        B, N = (2, 256)
        init = lambda k, shape: jax.random.normal(k, shape, jnp.float32) * 0.02
        return {'x': jax.random.normal(ks[0], (B, N, DIM), jnp.float32), 'Wqkv': init(ks[1], (DEPTH, DIM, 3 * INNER)), 'q_scale': jnp.ones((DEPTH, DIM_HEAD), jnp.float32), 'k_scale': jnp.ones((DEPTH, DIM_HEAD), jnp.float32), 'Wo': init(ks[2], (DEPTH, INNER, DIM)), 'ln_g': jnp.ones((DEPTH, DIM), jnp.float32), 'ln_b': jnp.zeros((DEPTH, DIM), jnp.float32), 'W1': init(ks[3], (DEPTH, DIM, 2 * DIM_INNER)), 'b1': jnp.zeros((DEPTH, 2 * DIM_INNER), jnp.float32), 'W2': init(ks[4], (DEPTH, DIM_INNER, DIM)), 'b2': jnp.zeros((DEPTH, DIM), jnp.float32)}
    _L0_ffn_in = _L0_ffn_setup()
    _d = {'L0_attn_x': _L0_attn_in['x'], 'L0_attn_Wq': _L0_attn_in['Wq'], 'L0_attn_bq': _L0_attn_in['bq'], 'L0_attn_Wdown': _L0_attn_in['Wdown'], 'L0_attn_bdown': _L0_attn_in['bdown'], 'L0_attn_Wup': _L0_attn_in['Wup'], 'L0_attn_bup': _L0_attn_in['bup'], 'L0_attn_Wout': _L0_attn_in['Wout'], 'L0_attn_bout': _L0_attn_in['bout'], 'L0_ffn_Wqkv': _L0_ffn_in['Wqkv'], 'L0_ffn_q_scale': _L0_ffn_in['q_scale'], 'L0_ffn_k_scale': _L0_ffn_in['k_scale'], 'L0_ffn_Wo': _L0_ffn_in['Wo'], 'L0_ffn_ln_g': _L0_ffn_in['ln_g'], 'L0_ffn_ln_b': _L0_ffn_in['ln_b'], 'L0_ffn_W1': _L0_ffn_in['W1'], 'L0_ffn_b1': _L0_ffn_in['b1'], 'L0_ffn_W2': _L0_ffn_in['W2'], 'L0_ffn_b2': _L0_ffn_in['b2']}
    _x0 = _d['L0_attn_x']
    _d['L0_attn_x'] = jax.random.normal(jax.random.fold_in(jax.random.key(seed), 1), (4, 512, 128), dtype=_x0.dtype)
    del _x0
    return _d

def reference(L0_attn_x, L0_attn_Wq, L0_attn_bq, L0_attn_Wdown, L0_attn_bdown, L0_attn_Wup, L0_attn_bup, L0_attn_Wout, L0_attn_bout, L0_ffn_Wqkv, L0_ffn_q_scale, L0_ffn_k_scale, L0_ffn_Wo, L0_ffn_ln_g, L0_ffn_ln_b, L0_ffn_W1, L0_ffn_b1, L0_ffn_W2, L0_ffn_b2):

    def _L0_attn_ref(x, Wq, bq, Wdown, bdown, Wup, bup, Wout, bout):
        import jax, jax.numpy as jnp
        import numpy as np
        D_MODEL = 128
        N_HEADS = 16
        D_LATENT = 32
        HEAD_DIM = D_MODEL // N_HEADS

        def apply_rope(x):
            B, T, H, D = x.shape
            inv_freq = 1.0 / 10000.0 ** (jnp.arange(0, D, 2, dtype=jnp.float32) / D)
            t = jnp.arange(T, dtype=jnp.float32)
            freqs = t[:, None] * inv_freq[None, :]
            sin_f = jnp.sin(freqs)[None, :, None, :]
            cos_f = jnp.cos(freqs)[None, :, None, :]
            x1, x2 = jnp.split(x, 2, axis=-1)
            return jnp.concatenate([x1 * cos_f - x2 * sin_f, x1 * sin_f + x2 * cos_f], axis=-1)
        B, T, D = x.shape
        H, Dh = (N_HEADS, HEAD_DIM)
        q = x @ Wq + bq
        kv_latent = x @ Wdown + bdown
        kv = kv_latent @ Wup + bup
        q = q.reshape(B, T, H, Dh)
        kv = kv.reshape(B, T, H, 2 * Dh)
        k, v = jnp.split(kv, 2, axis=-1)
        q = apply_rope(q)
        k = apply_rope(k)
        att = jnp.einsum('bthd,btgd->bthg', q, k) / jnp.sqrt(jnp.float32(Dh))
        att = jax.nn.softmax(att, axis=-1)
        out = jnp.einsum('bthg,btgd->bthd', att, v)
        out = out.reshape(B, T, D)
        return out @ Wout + bout

    def _L0_ffn_ref(x, Wqkv, q_scale, k_scale, Wo, ln_g, ln_b, W1, b1, W2, b2):
        import jax, jax.numpy as jnp
        import numpy as np
        DIM = 128
        DEPTH = 6
        HEADS = 16
        DIM_HEAD = 64
        WINDOW = 32
        INNER = HEADS * DIM_HEAD
        DIM_INNER = int(DIM * 4 * 2 / 3)
        QK_SCALE = 8.0

        def shift_tokens(t):
            a, s = jnp.split(t, 2, -1)
            s = jnp.pad(s, ((0, 0), (1, 0), (0, 0)))[:, :-1]
            return jnp.concatenate([a, s], -1)

        def l2norm(t):
            return t / jnp.maximum(jnp.linalg.norm(t, axis=-1, keepdims=True), 1e-12)

        def rotate_half(x):
            x1, x2 = jnp.split(x, 2, -1)
            return jnp.concatenate([-x2, x1], -1)

        def rotary_tables(n):
            half = jnp.arange(0, DIM_HEAD, 2, dtype=jnp.float32)
            inv_freq = 1.0 / 10000.0 ** (half / DIM_HEAD)
            t = jnp.arange(n, dtype=jnp.float32)
            freqs = t[:, None] * inv_freq[None, :]
            freqs = jnp.concatenate([freqs, freqs], -1)
            base_scale = (half + 0.4 * DIM_HEAD) / (1.4 * DIM_HEAD)
            power = (t - n // 2) / (WINDOW // 2)
            scale = base_scale[None, :] ** power[:, None]
            scale = jnp.concatenate([scale, scale], -1)
            return (freqs, scale)

        def local_attention(q, k, v):
            b, h, n, d = q.shape
            w = WINDOW
            nw = n // w
            bq = q.reshape(b, h, nw, w, d)
            bk = k.reshape(b, h, nw, w, d)
            bv = v.reshape(b, h, nw, w, d)

            def look(t):
                p = jnp.pad(t, ((0, 0), (0, 0), (1, 0), (0, 0), (0, 0)))
                return jnp.concatenate([p[:, :, :nw], p[:, :, 1:]], axis=3)
            bk2, bv2 = (look(bk), look(bv))
            seq = jnp.arange(n).reshape(nw, w)
            seq_p = jnp.pad(seq, ((1, 0), (0, 0)), constant_values=-1)
            jt = jnp.concatenate([seq_p[:nw], seq_p[1:]], axis=1)
            it = seq[:, :, None]
            jb = jt[:, None, :]
            mask = (it < jb) | (it > jb + w) | (jb == -1)
            sim = jnp.einsum('bhwie,bhwje->bhwij', bq, bk2) * QK_SCALE
            sim = jnp.where(mask, -jnp.finfo(sim.dtype).max, sim)
            attn = jax.nn.softmax(sim, -1)
            out = jnp.einsum('bhwij,bhwje->bhwie', attn, bv2)
            return out.reshape(b, h, n, d)

        def attn_layer(x, Wqkv, qs, ksc, Wo):
            b, n, _ = x.shape
            qkv = x @ Wqkv
            q, k, v = jnp.split(qkv, 3, -1)
            sh = lambda t: t.reshape(b, n, HEADS, DIM_HEAD).transpose(0, 2, 1, 3)
            q, k, v = (sh(q), sh(k), sh(v))
            q = l2norm(q) * qs
            k = l2norm(k) * ksc
            freqs, scale = rotary_tables(n)
            cos, sin = (jnp.cos(freqs), jnp.sin(freqs))
            q = q * cos * scale + rotate_half(q) * sin * scale
            inv = 1.0 / scale
            k = k * cos * inv + rotate_half(k) * sin * inv
            out = local_attention(q, k, v)
            out = out.transpose(0, 2, 1, 3).reshape(b, n, INNER)
            return out @ Wo

        def ffn_layer(x, g, bln, W1, b1, W2, b2):
            mu = x.mean(-1, keepdims=True)
            var = ((x - mu) ** 2).mean(-1, keepdims=True)
            xn = (x - mu) / jnp.sqrt(var + 1e-05) * g + bln
            hg = xn @ W1 + b1
            a, gate = jnp.split(hg, 2, -1)
            return a * jax.nn.gelu(gate, approximate=False) @ W2 + b2
        for i in range(DEPTH):
            x = attn_layer(shift_tokens(x), Wqkv[i], q_scale[i], k_scale[i], Wo[i]) + x
            x = ffn_layer(shift_tokens(x), ln_g[i], ln_b[i], W1[i], b1[i], W2[i], b2[i]) + x
        return x
    x = L0_attn_x
    xn = _layernorm(x, axis=-1)
    x = x + _L0_attn_ref(xn, L0_attn_Wq, L0_attn_bq, L0_attn_Wdown, L0_attn_bdown, L0_attn_Wup, L0_attn_bup, L0_attn_Wout, L0_attn_bout) + _L0_ffn_ref(xn, L0_ffn_Wqkv, L0_ffn_q_scale, L0_ffn_k_scale, L0_ffn_Wo, L0_ffn_ln_g, L0_ffn_ln_b, L0_ffn_W1, L0_ffn_b1, L0_ffn_W2, L0_ffn_b2)
    return x

_drawn_inputs = setup_inputs


def setup_inputs(seed=0):
    import zlib

    import numpy as np

    out = dict(_drawn_inputs(seed))
    spreads = {'L0_attn_bq': (0.0, 1.504),
     'L0_attn_bdown': (0.0, 0.912),
     'L0_attn_bup': (0.0, 0.935),
     'L0_attn_bout': (0.0, 0.488),
     'L0_ffn_q_scale': (1.0, 0.6),
     'L0_ffn_k_scale': (1.0, 0.6),
     'L0_ffn_ln_g': (1.0, 0.6),
     'L0_ffn_ln_b': (0.0, 0.8),
     'L0_ffn_b1': (0.0, 0.8),
     'L0_ffn_b2': (0.0, 0.1)}
    factors = {'L0_ffn_W1': 3.7, 'L0_ffn_W2': 3.631}
    for name, (base, spread) in spreads.items():
        noise = np.random.default_rng([zlib.crc32(name.encode()), seed]).standard_normal(out[name].shape)
        drawn = base * np.exp(spread * noise) if base else spread * noise
        out[name] = jnp.asarray(drawn.astype(out[name].dtype))
    for name, factor in factors.items():
        out[name] = (out[name] * factor).astype(out[name].dtype)
    return out
```

```python
from contextlib import ExitStack

import concourse.bass as bass
from concourse import mybir

F32 = mybir.dt.float32
BF16 = mybir.dt.bfloat16
I32 = mybir.dt.int32
ALU = mybir.AluOpType
ACT = mybir.ActivationFunctionType
AXX = mybir.AxisListType.X

P = 128
B, T, D = 4, 512, 128
TILES = T // P
AH, AD, AL = 16, 8, 32
L, H, E, W = 6, 16, 64, 32
PAIRS = H // 2
WT = P // W
INNER = H * E
F = int(D * 4 * 2 / 3)
FC = -(-F // P)
FREM = F - (FC - 1) * P
NEG = -1e30
EPS = 1e-5
RSQRT_MAGIC = 0x5F3759DF
C_ID, C_MASK, C_MASK0, C_END = 0, P, P + 2 * W, P + 4 * W
V_G, V_B, V_A, V_GATE, V_B2, V_END = 0, 1, 2, 2 + FC, 2 + 2 * FC, 3 + 2 * FC
A_BOUT, A_BDOWN, A_END = 0, 1, 2

XD_SLOTS = TILES * WT + 2
XD_USES = -(-XD_SLOTS // 4)
XPAD = 3 * W
AFTER = [("p", -1, i) for i in range(2)] + [("y", -1, i) for i in range(4)]
FFN = [(k, c) for c in range(FC) for k in ("gate", "val")]
RING = (
    [("t", 0, i) for i in range(4)] + AFTER
    + [("xd", i) for i in range(XD_USES)]
    + [("t", 1, i) for i in range(4)] + [("p", 0, i) for i in range(2)] + [("y", 0, i) for i in range(4)]
    + [("t", 2, i) for i in range(4)] + [("xn",)] + [("p", 1, i) for i in range(2)] + [("y", 1, i) for i in range(4)]
    + FFN + [("t", 3, i) for i in range(4)] + [("p", 2, i) for i in range(2)] + [("y", 2, i) for i in range(4)]
)
RING_PREV = AFTER + [("xn",)] + FFN
RING_HALF = len(RING) // 2
assert len(RING) % 2 == 0
UNITS = L * B
NORM_STEPS = 11
LN_STEPS = 3 + NORM_STEPS
TILE_STEPS = 2 + NORM_STEPS
SOFT_STEPS = 2
A_STEPS = TILES * (2 + 1 + 1 + 1)


def program(nc, x, avec, abias, wq, wdown, wup, wout, wqkv, wvt, wo, w1, w2, fvec, qks, cst, atab, ftab, out):
    ctx = ExitStack()
    with ctx:
        def sbuf(name, shape, dt=F32, where=ctx):
            return where.enter_context(nc.sbuf_tensor(name, shape, dt))

        def sem(name):
            return ctx.enter_context(nc.semaphore(name))

        ps = ctx.enter_context(nc.psum_tensor("banks", [P, 8, 512], F32))
        xT = sbuf("xT", [P, B * T])
        accT = sbuf("accT", [P, B * T])
        consts = sbuf("consts", [P, C_END])
        ident = consts[:, C_ID:C_ID + P]
        identb = sbuf("identb", [P, P], BF16)
        maskb = sbuf("maskb", [P, 2, 2 * W], BF16)
        st6 = sbuf("st6", [P, B * TILES, 6])
        mv = sbuf("mv", [P, B * TILES, 2])
        spare = sbuf("spare", [P, 4])
        ss0 = sbuf("ss0", [P, B * TILES])
        ny = sbuf("ny", [P, 2 * H])
        nt = sbuf("nt", [P, 2 * H])

        aux = ExitStack()
        atb = sbuf("attn_tables", [P, 2, TILES, AD], F32, aux)
        avs = sbuf("avs", [P, A_END], F32, aux)
        abb = sbuf("attn_bias_rows", [P, 3 * P], F32, aux)
        wq_s = sbuf("wq_s", [P, P], F32, aux)
        wdn_s = sbuf("wdn_s", [P, AL], F32, aux)
        wup_s = sbuf("wup_s", [AL, 2 * P], F32, aux)
        wout_s = sbuf("wout_s", [P, D], F32, aux)
        xcur = sbuf("xcur", [P, T], F32, aux)
        lat = sbuf("lat", [AL, T], F32, aux)
        qkv = sbuf("qkv", [P, TILES, 3 * P], F32, aux)
        rsin = sbuf("rsin", [P, TILES, 2 * P], F32, aux)
        rqk = sbuf("rqk", [P, TILES, 2 * P], F32, aux)
        prodq = sbuf("prodq", [P, 2, AH * AH, AD], F32, aux)
        prodv = sbuf("prodv", [P, 2, P, AH], F32, aux)
        att = sbuf("att", [P, TILES, AH, AH], F32, aux)
        am = sbuf("am", [P, TILES, 3, AH], F32, aux)
        oraw = sbuf("oraw", [P, TILES, P], F32, aux)
        on = sbuf("on", [P, TILES, P], F32, aux)
        oT = sbuf("oT", [P, T], F32, aux)
        xn0 = sbuf("xn0", [P, B * TILES, D], F32, aux)
        xtok = sbuf("xtok", [P, B * TILES, D], F32, aux)
        aux.close()

        wqk = sbuf("wqk", [P, 2 * INNER])
        wv_s = sbuf("wv_s", [P, PAIRS, D])
        wo_s = sbuf("wo_s", [P, PAIRS, D])
        mh = sbuf("mh", [P, 2, PAIRS, D])
        w1_s = sbuf("w1_s", [P, 2 * F])
        w2_s = sbuf("w2_s", [P, FC, D])
        fv = sbuf("fv", [P, V_END])
        qkvec = sbuf("qk_vec", [P, 4, E])
        tabb = sbuf("tab_base", [P, 4, TILES, E])
        tab = sbuf("tab", [P, 4, TILES, E])
        xsa = sbuf("xsa", [P, XPAD + T + 2 * W])
        xsf = sbuf("xsf", [P, T])
        xd = sbuf("xd", [P, XD_SLOTS, D])
        sq = sbuf("sq", [P, 2 * H, E])
        qn = sbuf("qn", [P, 2, 2 * H, E])
        rot = sbuf("rot", [P, 2, 2 * H, E])
        ms = sbuf("ms", [P, 2 * H, E])
        qT = sbuf("qT", [P, 2, PAIRS, P])
        kT = sbuf("kT", [P, PAIRS, W + T])
        ss = sbuf("ss", [P, 2 * H])
        negm = sbuf("negm", [P, 2 * PAIRS])
        psum_ = sbuf("prob_sum", [P, 2 * PAIRS])
        rinv = sbuf("rinv", [P, 2, 2 * PAIRS])
        sm = sbuf("sm", [P, 2, 2 * PAIRS, 2 * W])
        pn = sbuf("pn", [P, PAIRS, 2, 2 * W])
        pT = sbuf("pT", [P, 2, PAIRS, P])
        yT = sbuf("yT", [P, 2, PAIRS, T])
        x1 = sbuf("x1", [P, T])
        xn = sbuf("xn", [P, TILES, D])
        xnT = sbuf("xnT", [P, T])
        ytok = rot[:, 0, :, :].rearrange("p h e -> p (h e)").rearrange("p (n d) -> p n d", d=D)
        gl = sbuf("gl", [P, FC, T])
        hT = gl

        names = """x_loaded const_loaded a_loaded pool_ready casts pro_chain xn0_ready pro_full pro_used x_done
        xcur_ready lat_full lat_ready a_full a_chain a_rot a_qk a_sub a_exp a_pvd a_pvp a_sum a_o ot_full ot_ready at_full acc_done
        mw_loaded qkv_loaded wqk_loaded ffn_loaded tabb_loaded m_full m_ready tab_ready ln_full
        xsa_ready xsf_ready qk_full sq_ready qn_ready xn_ready rotc_done ms_ready rot_ready
        sc_full sc_used p_ready rinv_ready pn_ready attn_full x1_ready out_full
        norm_chain soft_chain ln_chain sum_ready fin_full y_ready y_stored""".split()
        S = {n: sem(n) for n in names}
        ring_full = [sem("ring_full0"), sem("ring_full1")]
        ring_free = [sem("ring_free0"), sem("ring_free1")]

        def wait(eng, semaphore, count):
            if not (isinstance(count, int) and count <= 0):
                eng.wait_ge(semaphore, count)

        def ring_use(v, key):
            i = RING.index(key)
            r = i % 2
            if isinstance(v, int) and v == 0:
                return r, sum(k not in RING_PREV for k in RING[r:i:2])
            skipped = sum(k in RING_PREV for k in RING[r::2])
            if isinstance(v, int) and v == UNITS:
                return r, v * RING_HALF - skipped + sum(k in RING_PREV for k in RING[r:i:2])
            return r, v * RING_HALF + (i // 2 - skipped)

        def ring_take(v, key):
            r, n = ring_use(v, key)
            wait(nc.tensor, ring_free[r], n)
            return ps[:, 4 + r, :], ring_full[r]

        def ring_read(eng, v, key):
            r, n = ring_use(v, key)
            eng.wait_ge(ring_full[r], n + 1)
            return ps[:, 4 + r, :], ring_free[r]

        def ring_emptied(eng, v, *keys):
            for key in keys:
                r, n = ring_use(v, key)
                eng.wait_ge(ring_free[r], n + 1)

        def run_turns(eng, turn, first_layer_use, after):
            def inner(l):
                with eng.Fori(1, B - 1) as b:
                    turn(l * B + b, l, b, (l, b - 1), (l, b + 1))
            turn(0, 0, 0, None, (0, 1))
            with eng.Fori(0, L - 1) as l:
                first_layer_use(l)
                inner(l)
                turn(l * B + (B - 1), l, B - 1, (l, B - 2), (l + 1, 0))
                turn(l * B + B, l + 1, 0, (l, B - 1), (l + 1, 1))
            first_layer_use(L - 1)
            inner(L - 1)
            turn(UNITS - 1, L - 1, B - 1, (L - 1, B - 2), None)
            after()

        def pv_operands(t, half):
            h0, n = half * AH // 2, AH // 2
            o = prodv[:, t % 2, :, :].rearrange("p (h d) g -> p h d g", d=AD)[:, h0:h0 + n, :, :]
            probs = att[:, t, h0:h0 + n, :].unsqueeze(2).to_broadcast([P, n, AD, AH])
            values = qkv[:, t, 2 * P:3 * P].rearrange("p (d g) -> p d g", g=AH).unsqueeze(1).to_broadcast([P, n, AD, AH])
            return o, probs, values

        block = ctx.enter_context(nc.Block())

        @block.sync
        def _(sp):
            sp.dma_start(xtok[:, :, :], x.rearrange("b (n p) d -> p (b n) d", p=P)).then_inc(S["x_loaded"], 16)
            sp.dma_start(consts[:, :], cst).then_inc(S["const_loaded"], 16)
            for dst, src in ((avs[:, :], avec), (wq_s[:, :], wq), (wdn_s[:, :], wdown), (wup_s[:, :], wup),
                             (abb[:, :], abias.rearrange("(a n) -> a n", a=1).to_broadcast([P, 3 * P])),
                             (atb[:, :, :, :], atab), (wout_s[:, :], wout)):
                sp.dma_start(dst, src).then_inc(S["a_loaded"], 16)
            sp.wait_ge(S["acc_done"], B)
            sp.dma_start(tabb[:, :, :, :], ftab).then_inc(S["tabb_loaded"], 16)

            def load_layer(l):
                layer = lambda a: a[bass.ds(l, 1)]
                wait(sp, S["tab_ready"], l * 4)
                sp.dma_start(qkvec[:, :, :], layer(qks).to_broadcast([P, 4, E])).then_inc(S["qkv_loaded"], 16)
                wait(sp, S["qk_full"], l * (B * TILES))
                sp.dma_start(wqk[:, :], wqkv[bass.ds(l, 1), :, 0:2 * INNER].rearrange("l k n -> k (l n)")).then_inc(S["wqk_loaded"], 16)
                wait(sp, S["m_ready"], l)
                sp.dma_start(wv_s[:, :, :], layer(wvt).rearrange("l (p k) c -> k (l p) c", k=P)).then_inc(S["mw_loaded"], 16)
                sp.dma_start(wo_s[:, :, :], layer(wo).rearrange("l (p k) c -> k (l p) c", k=P)).then_inc(S["mw_loaded"], 16)
                sp.wait_ge(S["x_done"], l * B + B)
                sp.dma_start(w1_s[:, :], layer(w1).rearrange("l k n -> k (l n)")).then_inc(S["ffn_loaded"], 16)
                sp.dma_start(w2_s[:, :, :], layer(w2).rearrange("l (c k) n -> k (l c) n", k=P)).then_inc(S["ffn_loaded"], 16)
                sp.dma_start(fv[:, :], layer(fvec).rearrange("l k n -> k (l n)")).then_inc(S["ffn_loaded"], 16)

            load_layer(0)
            with sp.Fori(1, L) as l:
                load_layer(l)
            sp.wait_ge(S["x_done"], B + L * B)
            sp.dma_start(ytok, x.rearrange("b (n p) d -> p (b n) d", p=P)).then_inc(S["x_loaded"], 16)
            for b in range(B):
                sp.wait_ge(S["y_ready"], b + 1)
                sp.dma_start(out[b].rearrange("(n p) d -> p n d", p=P), ytok[:, b * TILES:(b + 1) * TILES, :]).then_inc(S["y_stored"], 16)
            sp.wait_ge(S["y_stored"], 16 * B)

        @block.tensor
        def _(pe):
            mm, tr = nc.tensor.matmul, nc.tensor.transpose
            pe.wait_ge(S["const_loaded"], 16)
            for b in range(B):
                pe.wait_ge(S["xn0_ready"], b + 1)
                for t in range(TILES):
                    last = tr(ps[:, b, t * P:(t + 1) * P], xn0[:, b * TILES + t, :], ident)
                last.then_inc(S["pro_full"], 1)
            pe.wait_ge(S["x_done"], B)
            pe.wait_ge(S["a_loaded"], 7 * 16)

            with pe.Fori(0, B) as b:
                pe.wait_ge(S["xcur_ready"], b + 1)
                mm(ps[0:AL, 4, :], wdn_s[:, :], xcur[:, :], start=True, stop=True).then_inc(S["lat_full"], 1)
                pe.wait_ge(S["lat_ready"], b + 1)
                pe.wait_ge(S["a_o"], b * TILES)
                for t in range(TILES):
                    c = slice(t * P, (t + 1) * P)
                    mm(ps[:, t, 0:P], xcur[:, c], wq_s[:, :], start=True, stop=True)
                    mm(ps[:, t, P:3 * P], lat[:, c], wup_s[:, :], start=True, stop=True).then_inc(S["a_full"], 1)
                pe.wait_ge(S["a_o"], b * TILES + TILES)
                for t in range(TILES):
                    last = tr(ps[:, 5, t * P:(t + 1) * P], on[:, t, :], ident)
                last.then_inc(S["ot_full"], 1)
                pe.wait_ge(S["ot_ready"], b + 1)
                pe.wait_ge(S["acc_done"], b)
                mm(ps[:, 6, :], wout_s[:, :], oT[:, :], start=True, stop=True).then_inc(S["at_full"], 1)

            pe.wait_ge(S["acc_done"], B)
            pe.wait_ge(S["casts"], 3)
            pe.wait_ge(S["pool_ready"], 3)

            def proj(v, l, t, n0=0, n1=4):
                if n0 == 0:
                    pe.wait_ge(S["wqk_loaded"], l * 16 + 16)
                    if t in (0, TILES):
                        pe.wait_ge(S["xsa_ready"], v + 1 + t // TILES)
                    wait(pe, S["qn_ready"], v * TILES + t)
                c = XPAD + (t % TILES) * P
                for n in range(n0, n1):
                    last = mm(ps[:, n, :], xsa[:, c:c + P], wqk[:, n * 512:(n + 1) * 512], start=True, stop=True)
                if n1 == 4:
                    last.then_inc(S["qk_full"], 1)

            def window_tokens(v):
                for i in range(XD_USES):
                    bank, full = ring_take(v, ("xd", i))
                    for j in range(min(4, XD_SLOTS - 4 * i)):
                        c = (4 * i + j) * W
                        last = tr(bank[:, j * P:(j + 1) * P], xsa[:, c:c + P], ident)
                    last.then_inc(full, 1)

            def to_features(v, t, i0, i1):
                r = rot[:, t % 2, :, :].rearrange("p h e -> p (h e)")
                for i in range(i0, i1):
                    if i % 2 == 0:
                        pe.wait_ge(S["rot_ready"], (v * TILES + t) * 2 + i // 2 + 1)
                    bank, full = ring_take(v, ("t", t, i))
                    for j in range(4):
                        c = 4 * i + j
                        last = tr(bank[:, j * P:(j + 1) * P], r[:, c * P:(c + 1) * P], ident)
                    last.then_inc(full, 1)

            def local_scores(v, t, prev):
                wait(pe, S["sc_used"], v * TILES + t)
                ring_emptied(pe, v, ("t", t, 2), ("t", t, 3))
                if prev and t == 1:
                    pe.wait_ge(S["x1_ready"], v)
                if prev and t == 2:
                    pe.wait_ge(S["xn_ready"], v)
                if prev and t == 3:
                    pe.wait_ge(S["x_done"], v + B)
                mk = maskb[:, 1 if t == 0 else 0, :].unsqueeze(1).to_broadcast([P, PAIRS, 2 * W])
                for e in range(2):
                    mm(ps[:, 6 + e, :], identb[:, :], mk, start=True, stop=False, skip_group_check=True)
                for p in range(PAIRS):
                    for i in range(WT):
                        w = t * WT + i
                        for e in range(2):
                            last = mm(ps[W * i:W * i + W, 6 + e, p * 2 * W:(p + 1) * 2 * W],
                                      qT[64 * e:64 * e + 64, t % 2, p, W * i:W * i + W],
                                      kT[64 * e:64 * e + 64, p, W * w:W * w + 2 * W],
                                      start=False, stop=(p == PAIRS - 1), skip_group_check=True)
                last.then_inc(S["sc_full"], 1)

            def probs_to_keys(v, t):
                pe.wait_ge(S["pn_ready"], v * TILES + t + 1)
                for i in range(2):
                    bank, full = ring_take(v, ("p", t, i))
                    for j in range(4):
                        last = tr(bank[:, j * P:(j + 1) * P], pn[:, 4 * i + j, :, :].rearrange("q e k -> q (e k)"), ident)
                    last.then_inc(full, 1)

            def weigh_tokens(v, t):
                ring_emptied(pe, v, ("p", t, 0), ("p", t, 1))
                for wp in range(2):
                    for e in range(2):
                        bank, full = ring_take(v, ("y", t, 2 * wp + e))
                        for i in range(2):
                            wi = 2 * wp + i
                            last = mm(bank[:, i * 256:(i + 1) * 256], xd[64 * e:64 * e + 64, (t % TILES) * WT + wi + 2 * (1 - e), :],
                                      pT[64 * e:64 * e + 64, t % 2, :, W * wi:W * wi + W], start=True, stop=True)
                        last.then_inc(full, 1)

            def attention_out(v, l, e, p0=0, p1=PAIRS):
                if e == 0:
                    pe.wait_ge(S["m_ready"], l + 1)
                    ring_emptied(pe, v, ("y", -1, 2), ("y", -1, 3))
                    pe.wait_ge(S["sc_used"], UNITS * TILES if isinstance(v, int) and v == UNITS else v * TILES + 1)
                for p in range(p0, p1):
                    last = mm(ps[:, 7, :], mh[:, e, p, :], yT[:, e, p, :], start=(e + p == 0), stop=(e == 1 and p == PAIRS - 1))
                if e == 1 and p1 == PAIRS:
                    last.then_inc(S["attn_full"], 1)

            def to_tokens(v):
                pe.wait_ge(S["xsf_ready"], v)
                if not (isinstance(v, int) and v == UNITS):
                    pe.wait_ge(S["sc_used"], v * TILES + 2)
                for t in range(TILES):
                    last = tr(ps[:, 7, t * P:(t + 1) * P], xsf[:, t * P:(t + 1) * P], ident)
                last.then_inc(S["ln_full"], 1)

            def normed_to_features(v):
                pe.wait_ge(S["xn_ready"], v)
                bank, full = ring_take(v, ("xn",))
                for t in range(TILES):
                    last = tr(bank[:, t * P:(t + 1) * P], xn[:, t, :], ident)
                last.then_inc(full, 1)

            def widen(v, l, c):
                if c == 0:
                    pe.wait_ge(S["ffn_loaded"], l * 48 + 48)
                    ring_emptied(pe, v, ("xn",))
                m = P if c < FC - 1 else FREM
                for key, c0 in (("gate", F), ("val", 0)):
                    bank, full = ring_take(v, (key, c))
                    mm(bank[0:m, :], w1_s[:, c0 + c * P:c0 + c * P + m], xnT[:, :], start=True, stop=True).then_inc(full, 1)

            def narrow(v):
                if not (isinstance(v, int) and v == UNITS):
                    pe.wait_ge(S["sc_used"], v * TILES + 3)
                for c in range(FC):
                    m = P if c < FC - 1 else FREM
                    ring_emptied(pe, v, ("val", c))
                    last = mm(ps[:, 6, :], w2_s[0:m, c, :], hT[0:m, c, :], start=(c == 0), stop=(c == FC - 1))
                last.then_inc(S["out_full"], 1)

            def turn(v, l, b, prev, nxt):
                if not (isinstance(b, int) and b == 0):
                    pe.wait_ge(S["m_ready"], l + 1)
                def start(t):
                    proj(v, l, t + 1, 0, 2)
                    to_features(v, t, 0, 2)
                    proj(v, l, t + 1, 2, 3)
                    to_features(v, t, 2, 3)
                    proj(v, l, t + 1, 3, 4)
                    to_features(v, t, 3, 4)

                start(0)
                if prev:
                    probs_to_keys(v, -1)
                local_scores(v, 0, prev)
                if prev:
                    weigh_tokens(v, -1)
                window_tokens(v)
                proj(v, l, 2)
                if prev:
                    attention_out(v, prev[0], 0)
                to_features(v, 1, 0, 2)
                if prev:
                    attention_out(v, prev[0], 1, 0, 2)
                to_features(v, 1, 2, 3)
                if prev:
                    attention_out(v, prev[0], 1, 2, 4)
                to_features(v, 1, 3, 4)
                if prev:
                    attention_out(v, prev[0], 1, 4, PAIRS)
                probs_to_keys(v, 0)
                local_scores(v, 1, prev)
                if not prev:
                    ring_emptied(pe, v, ("xd", XD_USES - 1))
                weigh_tokens(v, 0)
                if prev:
                    to_tokens(v)
                start(2)
                if prev:
                    normed_to_features(v)
                probs_to_keys(v, 1)
                local_scores(v, 2, prev)
                weigh_tokens(v, 1)
                for c in range(FC):
                    if prev:
                        widen(v, prev[0], c)
                    if nxt and c < 2:
                        proj(v, nxt[0], TILES, 2 * c, 2 * c + 2)
                to_features(v, 3, 0, 4)
                if prev:
                    narrow(v)
                probs_to_keys(v, 2)
                weigh_tokens(v, 2)
                local_scores(v, 3, prev)

            def build_m(l):
                pe.wait_ge(S["mw_loaded"], l * 32 + 32)
                pe.wait_ge(S["qn_ready"], l * (B * TILES) + (TILES + 1))
                for p in range(PAIRS):
                    for e in range(2):
                        last = mm(ps[:, 2 * e + p // 4, (p % 4) * D:(p % 4 + 1) * D], wv_s[64 * e:64 * e + 64, p, :],
                                  wo_s[64 * e:64 * e + 64, p, :], start=True, stop=True)
                last.then_inc(S["m_full"], 1)

            def after():
                probs_to_keys(UNITS, -1)
                weigh_tokens(UNITS, -1)
                attention_out(UNITS, L - 1, 0)
                attention_out(UNITS, L - 1, 1)
                to_tokens(UNITS)
                normed_to_features(UNITS)
                for c in range(FC):
                    widen(UNITS, L - 1, c)
                narrow(UNITS)

            proj(0, 0, 0)
            run_turns(pe, turn, build_m, after)
            pe.wait_ge(S["sum_ready"], 1)
            for b in range(B):
                for t in range(TILES):
                    last = tr(ps[:, b, t * P:(t + 1) * P], xT[:, b * T + t * P:b * T + (t + 1) * P], ident)
                last.then_inc(S["fin_full"], 1)

        @block.scalar
        def _(act):
            fn = nc.scalar.activation
            act.wait_ge(S["a_loaded"], 7 * 16)
            with act.Fori(0, B) as b:
                act.wait_ge(S["a_full"], b * TILES)
                act.wait_ge(S["x_done"], B)
                fn(xcur[:, :], xT[:, bass.ts(b, T)], ACT.Copy).then_inc(S["xcur_ready"], 1)
                act.wait_ge(S["lat_full"], b + 1)
                fn(lat[:, :], ps[0:AL, 4, :], ACT.Identity, bias=avs[0:AL, A_BDOWN:A_BDOWN + 1]).then_inc(S["lat_ready"], 1)
                for t in range(TILES):
                    act.wait_ge(S["a_sub"], b * TILES + t + 1)
                    fn(att[:, t, :, :], att[:, t, :, :], ACT.Exp, scale=float(AD) ** -0.5).then_inc(S["a_exp"], 1)
                act.wait_ge(S["ot_full"], b + 1)
                fn(oT[:, :], ps[:, 5, :], ACT.Copy).then_inc(S["ot_ready"], 1)
            act.wait_ge(S["acc_done"], B)
            act.wait_ge(S["pool_ready"], 3)

            def shift(dst, src, signal):
                fn(dst[0:64, :], src[0:64, :], ACT.Copy)
                fn(dst[64:P, 1:T], src[64:P, 0:T - 1], ACT.Copy).then_inc(signal, 1)

            def shift_input(v, b):
                act.wait_ge(S["x_done"], v + 1)
                wait(act, S["qk_full"], v * TILES)
                shift(xsa[:, XPAD:XPAD + T], xT[:, bass.ts(b, T)], S["xsa_ready"])

            def squares(v, t):
                act.wait_ge(S["qk_full"], v * TILES + t + 1)
                fn(sq[:, 0:H, :].rearrange("p h e -> p (h e)"), ps[:, 0:2, :], ACT.Square)
                fn(sq[:, H:2 * H, :].rearrange("p h e -> p (h e)"), ps[:, 2:4, :], ACT.Square).then_inc(S["sq_ready"], 1)

            def window_tokens(v):
                for i in range(XD_USES):
                    bank, free = ring_read(act, v, ("xd", i))
                    n = min(4, XD_SLOTS - 4 * i)
                    fn(xd[:, 4 * i:4 * i + n, :].rearrange("p w d -> p (w d)"), bank[:, 0:n * P], ACT.Copy).then_inc(free, 1)

            def features(v, t):
                for i in range(4):
                    bank, free = ring_read(act, v, ("t", t, i))
                    src = bank.rearrange("p (j q) -> p j q", q=P)
                    p0 = i % 2 * 4
                    dst = qT[:, t % 2, p0:p0 + 4, :] if i < 2 else kT[:, p0:p0 + 4, W + t * P:W + (t + 1) * P]
                    fn(dst, src, ACT.Copy).then_inc(free, 1)

            def exps(v, t):
                act.wait_ge(S["sc_used"], v * TILES + t + 1)
                fn(sm[:, t % 2, :, :], sm[:, t % 2, :, :], ACT.Exp).then_inc(S["p_ready"], 1)

            def probs(v, t):
                for i in range(2):
                    bank, free = ring_read(act, v, ("p", t, i))
                    fn(pT[:, t % 2, 4 * i:4 * i + 4, :], bank.rearrange("p (j q) -> p j q", q=P), ACT.Copy).then_inc(free, 1)

            def weighed(v, t):
                for i in range(4):
                    bank, free = ring_read(act, v, ("y", t, i))
                    c0 = (t % TILES) * P + i // 2 * 2 * W
                    fn(yT[:, i % 2, :, c0:c0 + 2 * W].rearrange("f p (i q) -> f i p q", q=W),
                       bank.rearrange("f (i p q) -> f i p q", p=PAIRS, q=W), ACT.Copy).then_inc(free, 1)

            def shift_middle(v):
                act.wait_ge(S["x1_ready"], v)
                shift(xsf[:, :], x1[:, :], S["xsf_ready"])

            def normed(v, l):
                act.wait_ge(S["ffn_loaded"], l * 48 + 48)
                bank, free = ring_read(act, v, ("xn",))
                fn(xnT[:, :], bank, ACT.Identity, scale=fv[:, V_G:V_G + 1], bias=fv[:, V_B:V_B + 1]).then_inc(free, 1)

            def gates(v):
                for c in range(FC):
                    m = P if c < FC - 1 else FREM
                    bank, free = ring_read(act, v, ("gate", c))
                    fn(gl[0:m, c, :], bank[0:m, :], ACT.Gelu, bias=fv[0:m, V_GATE + c:V_GATE + c + 1]).then_inc(free, 1)

            def turn(v, l, b, prev, nxt):
                features(v, 0)
                squares(v, 1)
                if prev:
                    probs(v, -1)
                    weighed(v, -1)
                window_tokens(v)
                exps(v, 0)
                squares(v, 2)
                features(v, 1)
                probs(v, 0)
                if prev:
                    shift_middle(v)
                weighed(v, 0)
                exps(v, 1)
                features(v, 2)
                squares(v, 3)
                if prev:
                    normed(v, prev[0])
                probs(v, 1)
                weighed(v, 1)
                if nxt:
                    shift_input(v + 1, nxt[1])
                exps(v, 2)
                if prev:
                    gates(v)
                if nxt:
                    squares(v, TILES)
                features(v, 3)
                probs(v, 2)
                weighed(v, 2)
                exps(v, 3)

            def copy_m(l):
                act.wait_ge(S["m_full"], l + 1)
                fn(mh[:, 0, :, :].rearrange("c p f -> c (p f)"), ps[:, 0:2, :], ACT.Copy)
                fn(mh[:, 1, :, :].rearrange("c p f -> c (p f)"), ps[:, 2:4, :], ACT.Copy).then_inc(S["m_ready"], 1)

            def after():
                probs(UNITS, -1)
                weighed(UNITS, -1)
                shift_middle(UNITS)
                normed(UNITS, L - 1)
                gates(UNITS)

            shift_input(0, 0)
            squares(0, 0)
            run_turns(act, turn, copy_m, after)

        @block.vector
        def _(dve):
            v = nc.vector

            class Steps:
                def __init__(self, sem_, base):
                    self.sem, self.base, self.n = sem_, base, 0

                def done(self, ins):
                    self.n += 1
                    ins.then_inc(self.sem, 1)
                    dve.wait_ge(self.sem, self.base + self.n)

            def rsqrt(step, src, n):
                y, t = ny[:, 0:n], nt[:, 0:n]
                step.done(v.tensor_scalar(t.bitcast(I32), src.bitcast(I32), 1, None, ALU.logical_shift_right))
                step.done(v.tensor_scalar(y.bitcast(I32), t.bitcast(I32), -1.0, float(RSQRT_MAGIC), ALU.mult, ALU.add))
                for _ in range(3):
                    step.done(v.scalar_tensor_tensor(out=t, in0=y, scalar=-0.5, in1=y, op0=ALU.mult, op1=ALU.mult))
                    step.done(v.tensor_tensor(t, t, src, ALU.mult))
                    step.done(v.scalar_tensor_tensor(out=y, in0=t, scalar=1.5, in1=y, op0=ALU.add, op1=ALU.mult))

            def layer_norm(step, source, n, place):
                for i in range(n):
                    last = v.bn_stats(st6[:, i, :], source(i))
                step.done(last)
                v.memset(spare[:, 0:1], 0.0)
                for i in range(n):
                    last = v.bn_aggr(mv[:, i, :], st6[:, i, :])
                step.done(last)
                step.done(v.tensor_scalar(ss[:, 0:n] if n <= TILES else ss0[:, 0:n], mv[:, 0:n, 1], EPS, None, ALU.add))
                rsqrt(step, ss[:, 0:n] if n <= TILES else ss0[:, 0:n], n)
                for i in range(n):
                    dst, signal = place(i)
                    ins = v.tensor_scalar(dst, source(i), mv[:, i, 0:1], ny[:, i:i + 1], ALU.subtract, ALU.mult)
                    if signal is not None:
                        ins.then_inc(signal, 1)

            dve.wait_ge(S["x_loaded"], 16)
            step = Steps(S["pro_chain"], 0)
            layer_norm(step, lambda i: xtok[:, i, :], B * TILES,
                       lambda i: (xn0[:, i, :], S["xn0_ready"] if i % TILES == TILES - 1 else None))
            dve.wait_ge(S["const_loaded"], 16)
            v.tensor_copy(identb[:, :], ident).then_inc(S["casts"], 1)
            v.tensor_copy(maskb[:, 0, :], consts[:, C_MASK:C_MASK + 2 * W]).then_inc(S["casts"], 1)
            v.tensor_copy(maskb[:, 1, :], consts[:, C_MASK0:C_MASK0 + 2 * W]).then_inc(S["casts"], 1)
            for b in range(B):
                dve.wait_ge(S["pro_full"], b + 1)
                v.tensor_copy(xT[:, b * T:(b + 1) * T], ps[:, b, :]).then_inc(S["x_done"], 1)

            dve.wait_ge(S["a_loaded"], 7 * 16)
            with dve.Fori(0, B) as b:
                step = Steps(S["a_chain"], b * A_STEPS)

                def rotate_qk(t):
                    dve.wait_ge(S["a_o"], b * TILES)
                    dve.wait_ge(S["a_full"], b * TILES + t + 1)
                    step.done(v.tensor_tensor(qkv[:, t, :], ps[:, t, 0:3 * P], abb[:, :], ALU.add))
                    def heads(a):
                        return a[:, t, 0:2 * P].rearrange("p (h d) -> p h d", d=AD)
                    def table(i, o, n):
                        return atb[:, i, t, o:o + n].unsqueeze(1).to_broadcast([P, 2 * AH, n])
                    v.tensor_tensor(heads(rqk), heads(qkv), table(0, 0, AD), ALU.mult)
                    n = AD // 2
                    for o, i in ((0, n), (n, 0)):
                        last = v.tensor_tensor(heads(rsin)[:, :, o:o + n], heads(qkv)[:, :, i:i + n], table(1, o, n), ALU.mult)
                    step.done(last)
                    v.tensor_tensor(rqk[:, t, :], rqk[:, t, :], rsin[:, t, :], ALU.add).then_inc(S["a_rot"], 1)

                def reduce_qk(t):
                    dve.wait_ge(S["a_qk"], b * TILES + t + 1)
                    step.done(v.tensor_reduce(att[:, t, :, :].rearrange("p h g -> p (h g)"), prodq[:, t % 2, :, :], AXX, ALU.add))
                    step.done(v.tensor_reduce(am[:, t, 0, :], att[:, t, :, :], AXX, ALU.max, negate=True))
                    v.tensor_tensor(att[:, t, :, :], att[:, t, :, :], am[:, t, 0, :].unsqueeze(2).to_broadcast([P, AH, AH]),
                                    ALU.add).then_inc(S["a_sub"], 1)

                def weigh_v(t):
                    dve.wait_ge(S["a_exp"], b * TILES + t + 1)
                    if t >= 2:
                        dve.wait_ge(S["a_o"], b * TILES + t - 1)
                    v.tensor_tensor(*pv_operands(t, 0), ALU.mult).then_inc(S["a_pvd"], 1)
                    step.done(v.tensor_reduce(am[:, t, 1, :], att[:, t, :, :], AXX, ALU.add))
                    v.reciprocal(am[:, t, 2, :], am[:, t, 1, :])
                    dve.wait_ge(S["a_pvd"], b * TILES + t + 1)
                    dve.wait_ge(S["a_pvp"], b * TILES + t + 1)
                    v.tensor_reduce(oraw[:, t, :], prodv[:, t % 2, :, :], AXX, ALU.add).then_inc(S["a_sum"], 1)
                    dve.wait_ge(S["a_sum"], b * TILES + t + 1)
                    v.tensor_tensor(on[:, t, :].rearrange("p (h d) -> p h d", d=AD), oraw[:, t, :].rearrange("p (h d) -> p h d", d=AD),
                                    am[:, t, 2, :].unsqueeze(2).to_broadcast([P, AH, AD]), ALU.mult).then_inc(S["a_o"], 1)

                for t in range(TILES + 2):
                    if t < TILES:
                        rotate_qk(t)
                    if 1 <= t <= TILES:
                        reduce_qk(t - 1)
                    if t >= 2:
                        weigh_v(t - 2)
                dve.wait_ge(S["at_full"], b + 1)
                v.tensor_scalar(accT[:, bass.ts(b, T)], ps[:, 6, :], avs[:, A_BOUT:A_BOUT + 1], None, ALU.add).then_inc(S["acc_done"], 1)
                assert step.n == A_STEPS, step.n

            v_ = nc.vector

            def normalise(v, t):
                step = Steps(S["norm_chain"], (v * TILES + t) * TILE_STEPS)
                dve.wait_ge(S["sq_ready"], v * TILES + t + 1)
                step.done(v_.tensor_reduce(ss[:, :], sq[:, :, :], AXX, ALU.add))
                step.done(v_.tensor_scalar(ss[:, :], ss[:, :], 1e-24, None, ALU.max))
                rsqrt(step, ss[:, :], 2 * H)
                assert step.n == TILE_STEPS
                for s in range(2):
                    last = v_.tensor_tensor(qn[:, t % 2, s * H:(s + 1) * H, :],
                                            ps[:, 2 * s:2 * s + 2, :].rearrange("p k (h e) -> p (k h) e", e=E),
                                            ny[:, s * H:(s + 1) * H].unsqueeze(2).to_broadcast([P, H, E]), ALU.mult)
                last.then_inc(S["qn_ready"], 1)

            def sine_terms(v, l, t):
                dve.wait_ge(S["qn_ready"], v * TILES + t + 1)
                dve.wait_ge(S["tab_ready"], l * 4 + 4)
                wait(dve, S["rot_ready"], (v * TILES + t) * 2)
                for s in range(2):
                    for half in range(2):
                        o, i = half * E // 2, (1 - half) * E // 2
                        last = v_.tensor_tensor(ms[:, s * H:(s + 1) * H, o:o + E // 2],
                                                qn[:, t % 2, s * H:(s + 1) * H, i:i + E // 2],
                                                tab[:, 2 * s + 1, t % TILES, o:o + E // 2].unsqueeze(1).to_broadcast([P, H, E // 2]), ALU.mult)
                    last.then_inc(S["ms_ready"], 1)

            def shift_scores(v, t):
                step = Steps(S["soft_chain"], (v * TILES + t) * SOFT_STEPS)
                wait(dve, S["sc_used"], v * TILES + t)
                dve.wait_ge(S["sc_full"], v * TILES + t + 1)
                sc = ps[:, 6:8, :].rearrange("p e (h k) -> p (e h) k", k=2 * W)
                step.done(v_.tensor_reduce(negm[:, :], sc, AXX, ALU.max, negate=True))
                v_.tensor_tensor(sm[:, t % 2, :, :], sc, negm[:, :].unsqueeze(2).to_broadcast([P, H, 2 * W]),
                                 ALU.add).then_inc(S["sc_used"], 1)

            def sum_probs(v, t):
                step = Steps(S["soft_chain"], (v * TILES + t) * SOFT_STEPS + 1)
                wait(dve, S["rinv_ready"], v * TILES + t)
                dve.wait_ge(S["p_ready"], v * TILES + t + 1)
                step.done(v_.tensor_reduce(psum_[:, :], sm[:, t % 2, :, :], AXX, ALU.add))
                v_.reciprocal(rinv[:, t % 2, :], psum_[:, :]).then_inc(S["rinv_ready"], 1)

            def middle(v, b):
                dve.wait_ge(S["attn_full"], v)
                dve.wait_ge(S["x_done"], v - 1 + B)
                v_.tensor_tensor(x1[:, :], ps[:, 7, :], xT[:, bass.ts(b, T)], ALU.add).then_inc(S["x1_ready"], 1)

            def norm_tokens(v):
                step = Steps(S["ln_chain"], (v - 1) * LN_STEPS)
                dve.wait_ge(S["ln_full"], v)
                dve.wait_ge(S["qn_ready"], UNITS * TILES if isinstance(v, int) and v == UNITS else v * TILES + 3)
                layer_norm(step, lambda i: ps[:, 7, i * P:(i + 1) * P], TILES,
                           lambda i: (xn[:, i, :], S["xn_ready"] if i == TILES - 1 else None))
                assert step.n == LN_STEPS
                dve.wait_ge(S["xn_ready"], v)

            def gated(v):
                for c in range(FC):
                    m = P if c < FC - 1 else FREM
                    ring_emptied(dve, v, ("gate", c))
                    bank, free = ring_read(dve, v, ("val", c))
                    v_.scalar_tensor_tensor(out=hT[0:m, c, :], in0=bank[0:m, :], scalar=fv[0:m, V_A + c:V_A + c + 1],
                                            in1=gl[0:m, c, :], op0=ALU.add, op1=ALU.mult).then_inc(free, 1)

            def finish(v, b):
                dve.wait_ge(S["out_full"], v)
                dve.wait_ge(S["x1_ready"], v)
                v_.scalar_tensor_tensor(out=xT[:, bass.ts(b, T)], in0=ps[:, 6, :], scalar=fv[:, V_B2:V_B2 + 1], in1=x1[:, :],
                                        op0=ALU.add, op1=ALU.add).then_inc(S["x_done"], 1)

            def turn(v, l, b, prev, nxt):
                normalise(v, 1)
                shift_scores(v, 0)
                sine_terms(v, l, 1)
                sum_probs(v, 0)
                normalise(v, 2)
                sine_terms(v, l, 2)
                if prev:
                    middle(v, prev[1])
                shift_scores(v, 1)
                sum_probs(v, 1)
                if prev:
                    norm_tokens(v)
                normalise(v, 3)
                shift_scores(v, 2)
                sine_terms(v, l, 3)
                sum_probs(v, 2)
                if prev:
                    gated(v)
                if nxt:
                    normalise(v, TILES)
                if prev:
                    finish(v, prev[1])
                if nxt:
                    sine_terms(v, nxt[0], TILES)
                shift_scores(v, 3)
                sum_probs(v, 3)

            def after():
                middle(UNITS, B - 1)
                norm_tokens(UNITS)
                gated(UNITS)
                finish(UNITS, B - 1)

            normalise(0, 0)
            sine_terms(0, 0, 0)
            run_turns(dve, turn, lambda l: None, after)

            dve.wait_ge(S["x_done"], B + L * B)
            v.tensor_tensor(xT[:, :], xT[:, :], accT[:, :], ALU.add).then_inc(S["sum_ready"], 1)
            for b in range(B):
                dve.wait_ge(S["fin_full"], b + 1)
                dve.wait_ge(S["x_loaded"], 32)
                tok = ytok[:, b * TILES:(b + 1) * TILES, :].rearrange("p n d -> p (n d)")
                v.tensor_tensor(tok, ps[:, b, :], tok, ALU.add).then_inc(S["y_ready"], 1)

        @block.gpsimd
        def _(pool):
            g = nc.gpsimd
            with pool.Fori(0, B) as b:
                for t in range(TILES + 2):
                    if t < TILES:
                        pool.wait_ge(S["a_rot"], b * TILES + t + 1)
                        pool.wait_ge(S["a_sub"], b * TILES + max(0, t - 1))
                        q = rqk[:, t, 0:P].rearrange("p (h d) -> p h d", d=AD).unsqueeze(2).to_broadcast([P, AH, AH, AD])
                        k = rqk[:, t, P:2 * P].rearrange("p (g d) -> p g d", d=AD).unsqueeze(1).to_broadcast([P, AH, AH, AD])
                        g.tensor_tensor(prodq[:, t % 2, :, :].rearrange("p (h g) d -> p h g d", g=AH), q, k,
                                        ALU.mult).then_inc(S["a_qk"], 1)
                    if t >= 2:
                        pool.wait_ge(S["a_exp"], b * TILES + t - 1)
                        pool.wait_ge(S["a_o"], b * TILES + max(0, t - 3))
                        g.tensor_tensor(*pv_operands(t - 2, 1), ALU.mult).then_inc(S["a_pvp"], 1)
            pool.wait_ge(S["acc_done"], B)
            g.memset(xsa[:, :], 0.0).then_inc(S["pool_ready"], 1)
            pool.wait_ge(S["pool_ready"], 1)
            g.memset(xsf[:, :], 0.0).then_inc(S["pool_ready"], 1)
            pool.wait_ge(S["pool_ready"], 2)
            g.memset(kT[:, :, 0:W], 0.0).then_inc(S["pool_ready"], 1)
            pool.wait_ge(S["pool_ready"], 3)
            pool.wait_ge(S["tabb_loaded"], 16)

            def tables(l):
                pool.wait_ge(S["qkv_loaded"], l * 16 + 16)
                wait(pool, S["ms_ready"], l * (B * TILES * 2))
                wait(pool, S["rotc_done"], l * (B * TILES * 2))
                for k in range(4):
                    g.tensor_tensor(tab[:, k, :, :], tabb[:, k, :, :], qkvec[:, k, :].unsqueeze(1).to_broadcast([P, TILES, E]),
                                    ALU.mult).then_inc(S["tab_ready"], 1)

            def rotate(v, l, t):
                pool.wait_ge(S["tab_ready"], l * 4 + 4)
                pool.wait_ge(S["qn_ready"], v * TILES + t + 1)
                for s in range(2):
                    heads = slice(s * H, (s + 1) * H)
                    n = (v * TILES + t) * 2 + s + 1
                    g.tensor_tensor(rot[:, t % 2, heads, :], qn[:, t % 2, heads, :],
                                    tab[:, 2 * s, t % TILES, :].unsqueeze(1).to_broadcast([P, H, E]), ALU.mult).then_inc(S["rotc_done"], 1)
                    pool.wait_ge(S["rotc_done"], n)
                    pool.wait_ge(S["ms_ready"], n)
                    g.tensor_tensor(rot[:, t % 2, heads, :], rot[:, t % 2, heads, :], ms[:, heads, :], ALU.add).then_inc(S["rot_ready"], 1)

            def divide(v, t, prev):
                pool.wait_ge(S["rinv_ready"], v * TILES + t + 1)
                if t or prev:
                    ring_emptied(pool, v, ("p", t - 1, 1))
                g.tensor_tensor(pn[:, :, :, :].rearrange("q p e k -> q e p k"),
                                sm[:, t % 2, :, :].rearrange("q (e p) k -> q e p k", e=2),
                                rinv[:, t % 2, :].rearrange("q (e p) -> q e p", e=2).unsqueeze(3)
                                .to_broadcast([P, 2, PAIRS, 2 * W]), ALU.mult).then_inc(S["pn_ready"], 1)

            def turn(v, l, b, prev, nxt):
                for t in range(TILES):
                    if t < TILES - 1:
                        rotate(v, l, t + 1)
                    elif nxt:
                        if isinstance(b, int) and b == B - 1:
                            tables(nxt[0])
                        rotate(v, nxt[0], TILES)
                    divide(v, t, prev)

            tables(0)
            rotate(0, 0, 0)
            run_turns(pool, turn, lambda l: None, lambda: None)


def constants():
    import numpy as np
    f = np.float32
    cst = np.zeros((P, C_END), f)
    cst[:, C_ID:C_ID + P] = np.eye(P)
    i, j = np.arange(P)[:, None] % W, np.arange(2 * W)[None]
    seen = (i <= j) & (j <= i + W)
    cst[:, C_MASK:C_MASK + 2 * W] = np.where(seen, 0, NEG)
    cst[:, C_MASK0:C_MASK0 + 2 * W] = np.where(seen & ((np.arange(P)[:, None] >= W) | (j >= W)), 0, NEG)
    t = np.arange(T, dtype=f)
    inv = (f(1) / f(10000) ** (np.arange(0, AD, 2, dtype=f) / f(AD))).astype(f)
    fr = t[:, None] * inv[None]
    c, s = np.cos(fr), np.sin(fr)
    tiled = lambda a: a.reshape(TILES, P, -1).transpose(1, 0, 2)
    atab = np.stack([tiled(np.concatenate(a, 1)) for a in ((c, c), (-s, s))], 1).astype(f)
    half = np.arange(0, E, 2, dtype=f)
    inv = (f(1) / f(10000) ** (half / f(E))).astype(f)
    fr = t[:, None] * inv[None]
    base = ((half + f(0.4 * E)) / f(1.4 * E)).astype(f)
    sc = base[None] ** ((t - T // 2) / f(W // 2))[:, None]
    c, s = np.cos(fr), np.sin(fr)
    both = lambda a, b: np.concatenate([a, b], 1)
    tabs = [both(8 * c * sc, 8 * c * sc), both(-8 * s * sc, 8 * s * sc), both(c / sc, c / sc), both(-s / sc, s / sc)]
    ftab = np.stack([tiled(a) for a in tabs], 1).astype(f)
    return cst, atab, ftab


def kernel(**inputs):
    import numpy as np
    import concourse.bacc as bacc
    from concourse.bass_utils import run_bass_kernel_spmd

    a = {k[3:]: np.asarray(v) for k, v in inputs.items()}
    swap64 = (np.arange(E) + E // 2) % E

    def column(*vs):
        return np.stack([np.concatenate([v, np.zeros(P - len(v), v.dtype)]) for v in vs], 1)

    wup, bup = (a[k].reshape(-1, AH, 2, AD) for k in ("attn_Wup", "attn_bup"))
    wup, bup = (np.concatenate([z[:, :, 0].reshape(-1, P), z[:, :, 1].transpose(0, 2, 1).reshape(-1, P)], 1) for z in (wup, bup))
    w2 = np.zeros((L, FC * P, D), a["ffn_W2"].dtype)
    w2[:, 0:F] = a["ffn_W2"]
    cuts = lambda v: [v[i:i + P] for i in range(0, F, P)]
    qs, ks = a["ffn_q_scale"], a["ffn_k_scale"]
    cst, atab, ftab = constants()
    arrays = {
        "x": a["attn_x"],
        "avec": column(a["attn_bout"], a["attn_bdown"]),
        "abias": np.concatenate([a["attn_bq"], bup[0]]),
        "wq": a["attn_Wq"],
        "wdown": a["attn_Wdown"],
        "wup": wup,
        "wout": a["attn_Wout"],
        "wqkv": a["ffn_Wqkv"],
        "wvt": a["ffn_Wqkv"][:, :, 2 * INNER:].transpose(0, 2, 1),
        "wo": a["ffn_Wo"],
        "w1": a["ffn_W1"],
        "w2": w2,
        "fvec": np.stack([column(a["ffn_ln_g"][i], a["ffn_ln_b"][i], *cuts(a["ffn_b1"][i, 0:F]), *cuts(a["ffn_b1"][i, F:]),
                                 a["ffn_b2"][i]) for i in range(L)]),
        "qks": np.stack([qs, qs[:, swap64], ks, ks[:, swap64]], 1),
        "cst": cst, "atab": atab, "ftab": ftab,
    }
    nc = bacc.Bacc("TRN2", target_bir_lowering=False, num_devices=1)
    arrays = {f"in_{k}": np.ascontiguousarray(v) for k, v in arrays.items()}
    args = [nc.dram_tensor(k, v.shape, mybir.dt.from_np(v.dtype), kind="ExternalInput").ap() for k, v in arrays.items()]
    y = nc.dram_tensor("out_0", (B, T, D), F32, kind="ExternalOutput").ap()
    program(nc, *args, y)
    r = run_bass_kernel_spmd(nc, [arrays], core_ids=[0])
    return r.results[0]["out_0"]
```

```python
from contextlib import ExitStack

import concourse.bass as bass
from concourse import mybir

F32 = mybir.dt.float32
BF16 = mybir.dt.bfloat16
I32 = mybir.dt.int32
ALU = mybir.AluOpType
ACT = mybir.ActivationFunctionType
AXX = mybir.AxisListType.X

P = 128
B, T, D = 4, 512, 128
TILES = T // P
AH, AD, AL = 16, 8, 32
L, H, E, W = 6, 16, 64, 32
PAIRS = H // 2
WT = P // W
INNER = H * E
F = int(D * 4 * 2 / 3)
FC = -(-F // P)
FREM = F - (FC - 1) * P
NEG = -1e30
EPS = 1e-5
RSQRT_MAGIC = 0x5F3759DF
C_ID, C_MASK, C_MASK0, C_END = 0, P, P + 2 * W, P + 4 * W
V_G, V_B, V_A, V_GATE, V_B2, V_END = 0, 1, 2, 2 + FC, 2 + 2 * FC, 3 + 2 * FC
A_BOUT, A_BDOWN, A_END = 0, 1, 2

XD_SLOTS = TILES * WT + 2
XD_USE = 3
XD_USES = XD_SLOTS // XD_USE
XPAD = 3 * W
AFTER = [("p", -1, i) for i in range(2)] + [("y", -1, i) for i in range(4)]
FFN = [(k, c) for c in range(FC) for k in ("gate", "val")]
RING = (
    [("t", 0, i) for i in range(4)] + AFTER
    + [("xd", i) for i in range(XD_USES)]
    + [("t", 1, i) for i in range(4)] + [("p", 0, i) for i in range(2)] + [("y", 0, 0), ("y", 0, 1), ("ln",), ("y", 0, 2), ("y", 0, 3)]
    + [("t", 2, i) for i in range(4)] + [("p", 1, i) for i in range(2)] + [("y", 1, i) for i in range(4)] + [("xn",)]
    + FFN[0:4] + [("t", 3, 0), ("t", 3, 1)] + FFN[4:] + [("t", 3, 2), ("t", 3, 3)]
    + [("p", 2, i) for i in range(2)] + [("y", 2, i) for i in range(4)]
)
RING_PREV = AFTER + [("ln",), ("xn",)] + FFN
RING_HALF = len(RING) // 2
assert len(RING) % 2 == 0
UNITS = L * B
NORM_STEPS = 11
LN_STEPS = 3 + NORM_STEPS
TILE_STEPS = 2 + NORM_STEPS
SOFT_STEPS = 2
A_STEPS = TILES * (2 + 1 + 1 + 1)


def program(nc, x, avec, abias, wq, wdown, wup, wout, wqkv, wvt, wo, w1, w2, fvec, qks, cst, atab, ftab, out):
    ctx = ExitStack()
    with ctx:
        def sbuf(name, shape, dt=F32, where=ctx):
            return where.enter_context(nc.sbuf_tensor(name, shape, dt))

        def sem(name):
            return ctx.enter_context(nc.semaphore(name))

        ps = ctx.enter_context(nc.psum_tensor("banks", [P, 8, 512], F32))
        xT = sbuf("xT", [P, B * T])
        accT = sbuf("accT", [P, B * T])
        consts = sbuf("consts", [P, C_END])
        ident = consts[:, C_ID:C_ID + P]
        identb = sbuf("identb", [P, P], BF16)
        maskb = sbuf("maskb", [P, 2, 2 * W], BF16)
        st6 = sbuf("st6", [P, B * TILES, 6])
        mv = sbuf("mv", [P, B * TILES, 2])
        spare = sbuf("spare", [P, 4])
        ss0 = sbuf("ss0", [P, B * TILES])
        ny = sbuf("ny", [P, 2 * H + TILES])
        nt = sbuf("nt", [P, 2 * H + TILES])

        aux = ExitStack()
        atb = sbuf("attn_tables", [P, 2, TILES, AD], F32, aux)
        avs = sbuf("avs", [P, A_END], F32, aux)
        abb = sbuf("attn_bias_rows", [P, 3 * P], F32, aux)
        wq_s = sbuf("wq_s", [P, P], F32, aux)
        wdn_s = sbuf("wdn_s", [P, AL], F32, aux)
        wup_s = sbuf("wup_s", [AL, 2 * P], F32, aux)
        wout_s = sbuf("wout_s", [P, D], F32, aux)
        xcur = sbuf("xcur", [P, T], F32, aux)
        lat = sbuf("lat", [AL, T], F32, aux)
        qkv = sbuf("qkv", [P, TILES, 3 * P], F32, aux)
        rsin = sbuf("rsin", [P, TILES, 2 * P], F32, aux)
        rqk = sbuf("rqk", [P, TILES, 2 * P], F32, aux)
        prodq = sbuf("prodq", [P, 2, AH * AH, AD], F32, aux)
        prodv = sbuf("prodv", [P, 2, P, AH], F32, aux)
        att = sbuf("att", [P, TILES, AH, AH], F32, aux)
        am = sbuf("am", [P, TILES, 3, AH], F32, aux)
        oraw = sbuf("oraw", [P, TILES, P], F32, aux)
        on = sbuf("on", [P, TILES, P], F32, aux)
        oT = sbuf("oT", [P, T], F32, aux)
        xn0 = sbuf("xn0", [P, B * TILES, D], F32, aux)
        xtok = sbuf("xtok", [P, B * TILES, D], F32, aux)
        aux.close()

        wqk = sbuf("wqk", [P, 2 * INNER])
        wv_s = sbuf("wv_s", [P, PAIRS, D])
        wo_s = sbuf("wo_s", [P, PAIRS, D])
        mh = sbuf("mh", [P, 2, PAIRS, D])
        w1_s = sbuf("w1_s", [P, 2 * F])
        w2_s = sbuf("w2_s", [P, FC, D])
        fv = sbuf("fv", [P, V_END])
        qkvec = sbuf("qk_vec", [P, 4, E])
        tabb = sbuf("tab_base", [P, 4, TILES, E])
        tab = sbuf("tab", [P, 4, TILES, E])
        xsa = sbuf("xsa", [P, XPAD + T + 2 * W])
        xsf = sbuf("xsf", [P, T])
        xd = sbuf("xd", [P, XD_SLOTS, D])
        sq = sbuf("sq", [P, 2 * H, E])
        qn = sbuf("qn", [P, 2, 2 * H, E])
        rot = sbuf("rot", [P, 2, 2 * H, E])
        ms = sbuf("ms", [P, 2 * H, E])
        qT = sbuf("qT", [P, 2, PAIRS, P])
        kT = sbuf("kT", [P, PAIRS, W + T])
        ss = sbuf("ss", [P, 2 * H + TILES])
        negm = sbuf("negm", [P, 2 * PAIRS])
        psum_ = sbuf("prob_sum", [P, 2 * PAIRS])
        rinv = sbuf("rinv", [P, 2, 2 * PAIRS])
        sm = sbuf("sm", [P, 2, 2 * PAIRS, 2 * W])
        pn = sbuf("pn", [P, PAIRS, 2, 2 * W])
        pT = sbuf("pT", [P, 2, PAIRS, P])
        yT = sbuf("yT", [P, 2, PAIRS, T])
        x1 = sbuf("x1", [P, T])
        xn = sbuf("xn", [P, TILES, D])
        xnT = sbuf("xnT", [P, T])
        ytok = rot[:, 0, :, :].rearrange("p h e -> p (h e)").rearrange("p (n d) -> p n d", d=D)
        gl = sbuf("gl", [P, FC, T])
        hT = gl

        names = """x_loaded const_loaded a_loaded pool_ready casts pro_chain xn0_ready pro_full pro_used x_done
        xcur_ready lat_full lat_ready a_full a_chain a_rot a_qk a_sub a_exp a_pvd a_pvp a_sum a_o ot_full ot_ready at_full acc_done
        mw_loaded qkv_loaded wqk_loaded ffn_loaded tabb_loaded m_full m_ready tab_ready
        xsa_ready xsf_ready qk_full sq_ready qn_ready xn_ready rotc_done ms_ready rot_ready
        sc_full sc_used p_ready rinv_ready pn_ready attn_full x1_ready out_full
        norm_chain soft_chain ln_chain sum_ready fin_full y_ready y_stored""".split()
        S = {n: sem(n) for n in names}
        ring_full = [sem("ring_full0"), sem("ring_full1")]
        ring_free = [sem("ring_free0"), sem("ring_free1")]

        def wait(eng, semaphore, count):
            if not (isinstance(count, int) and count <= 0):
                eng.wait_ge(semaphore, count)

        def ring_use(v, key):
            i = RING.index(key)
            r = i % 2
            if isinstance(v, int) and v == 0:
                return r, sum(k not in RING_PREV for k in RING[r:i:2])
            skipped = sum(k in RING_PREV for k in RING[r::2])
            if isinstance(v, int) and v == UNITS:
                return r, v * RING_HALF - skipped + sum(k in RING_PREV for k in RING[r:i:2])
            return r, v * RING_HALF + (i // 2 - skipped)

        def ring_take(v, key):
            r, n = ring_use(v, key)
            wait(nc.tensor, ring_free[r], n)
            return ps[:, 4 + r, :], ring_full[r]

        def ring_read(eng, v, key):
            r, n = ring_use(v, key)
            eng.wait_ge(ring_full[r], n + 1)
            return ps[:, 4 + r, :], ring_free[r]

        def ring_emptied(eng, v, *keys):
            for key in keys:
                r, n = ring_use(v, key)
                eng.wait_ge(ring_free[r], n + 1)

        def run_turns(eng, turn, first_layer_use, after):
            def inner(l):
                with eng.Fori(1, B - 1) as b:
                    turn(l * B + b, l, b, (l, b - 1), (l, b + 1))
            turn(0, 0, 0, None, (0, 1))
            with eng.Fori(0, L - 1) as l:
                first_layer_use(l)
                inner(l)
                turn(l * B + (B - 1), l, B - 1, (l, B - 2), (l + 1, 0))
                turn(l * B + B, l + 1, 0, (l, B - 1), (l + 1, 1))
            first_layer_use(L - 1)
            inner(L - 1)
            turn(UNITS - 1, L - 1, B - 1, (L - 1, B - 2), None)
            after()

        def pv_operands(t, half):
            h0, n = half * AH // 2, AH // 2
            o = prodv[:, t % 2, :, :].rearrange("p (h d) g -> p h d g", d=AD)[:, h0:h0 + n, :, :]
            probs = att[:, t, h0:h0 + n, :].unsqueeze(2).to_broadcast([P, n, AD, AH])
            values = qkv[:, t, 2 * P:3 * P].rearrange("p (d g) -> p d g", g=AH).unsqueeze(1).to_broadcast([P, n, AD, AH])
            return o, probs, values

        block = ctx.enter_context(nc.Block())

        @block.sync
        def _(sp):
            sp.dma_start(xtok[:, :, :], x.rearrange("b (n p) d -> p (b n) d", p=P)).then_inc(S["x_loaded"], 16)
            sp.dma_start(consts[:, :], cst).then_inc(S["const_loaded"], 16)
            for dst, src in ((avs[:, :], avec), (wq_s[:, :], wq), (wdn_s[:, :], wdown), (wup_s[:, :], wup),
                             (abb[:, :], abias.rearrange("(a n) -> a n", a=1).to_broadcast([P, 3 * P])),
                             (atb[:, :, :, :], atab), (wout_s[:, :], wout)):
                sp.dma_start(dst, src).then_inc(S["a_loaded"], 16)
            sp.wait_ge(S["acc_done"], B)
            sp.dma_start(tabb[:, :, :, :], ftab).then_inc(S["tabb_loaded"], 16)

            def load_layer(l):
                layer = lambda a: a[bass.ds(l, 1)]
                wait(sp, S["tab_ready"], l * 4)
                sp.dma_start(qkvec[:, :, :], layer(qks).to_broadcast([P, 4, E])).then_inc(S["qkv_loaded"], 16)
                wait(sp, S["qk_full"], l * (B * TILES * 2))
                sp.dma_start(wqk[:, :], wqkv[bass.ds(l, 1), :, 0:2 * INNER].rearrange("l k n -> k (l n)")).then_inc(S["wqk_loaded"], 16)
                wait(sp, S["m_ready"], l * 2)
                sp.dma_start(wv_s[:, :, :], layer(wvt).rearrange("l (p k) c -> k (l p) c", k=P)).then_inc(S["mw_loaded"], 16)
                sp.dma_start(wo_s[:, :, :], layer(wo).rearrange("l (p k) c -> k (l p) c", k=P)).then_inc(S["mw_loaded"], 16)
                sp.wait_ge(S["x_done"], l * B + B)
                sp.dma_start(w1_s[:, :], layer(w1).rearrange("l k n -> k (l n)")).then_inc(S["ffn_loaded"], 16)
                sp.dma_start(w2_s[:, :, :], layer(w2).rearrange("l (c k) n -> k (l c) n", k=P)).then_inc(S["ffn_loaded"], 16)
                sp.dma_start(fv[:, :], layer(fvec).rearrange("l k n -> k (l n)")).then_inc(S["ffn_loaded"], 16)

            load_layer(0)
            with sp.Fori(1, L) as l:
                load_layer(l)
            sp.wait_ge(S["x_done"], B + L * B)
            sp.dma_start(ytok, x.rearrange("b (n p) d -> p (b n) d", p=P)).then_inc(S["x_loaded"], 16)
            for b in range(B):
                sp.wait_ge(S["y_ready"], b + 1)
                sp.dma_start(out[b].rearrange("(n p) d -> p n d", p=P), ytok[:, b * TILES:(b + 1) * TILES, :]).then_inc(S["y_stored"], 16)
            sp.wait_ge(S["y_stored"], 16 * B)

        @block.tensor
        def _(pe):
            mm, tr = nc.tensor.matmul, nc.tensor.transpose
            pe.wait_ge(S["const_loaded"], 16)
            for b in range(B):
                pe.wait_ge(S["xn0_ready"], b + 1)
                for t in range(TILES):
                    last = tr(ps[:, b, t * P:(t + 1) * P], xn0[:, b * TILES + t, :], ident)
                last.then_inc(S["pro_full"], 1)
            pe.wait_ge(S["x_done"], B)
            pe.wait_ge(S["a_loaded"], 7 * 16)

            with pe.Fori(0, B) as b:
                pe.wait_ge(S["xcur_ready"], b + 1)
                mm(ps[0:AL, 4, :], wdn_s[:, :], xcur[:, :], start=True, stop=True).then_inc(S["lat_full"], 1)
                pe.wait_ge(S["lat_ready"], b + 1)
                pe.wait_ge(S["a_o"], b * TILES)
                for t in range(TILES):
                    c = slice(t * P, (t + 1) * P)
                    mm(ps[:, t, 0:P], xcur[:, c], wq_s[:, :], start=True, stop=True)
                    mm(ps[:, t, P:3 * P], lat[:, c], wup_s[:, :], start=True, stop=True).then_inc(S["a_full"], 1)
                pe.wait_ge(S["a_o"], b * TILES + TILES)
                for t in range(TILES):
                    last = tr(ps[:, 5, t * P:(t + 1) * P], on[:, t, :], ident)
                last.then_inc(S["ot_full"], 1)
                pe.wait_ge(S["ot_ready"], b + 1)
                pe.wait_ge(S["acc_done"], b)
                mm(ps[:, 6, :], wout_s[:, :], oT[:, :], start=True, stop=True).then_inc(S["at_full"], 1)

            pe.wait_ge(S["acc_done"], B)
            pe.wait_ge(S["casts"], 3)
            pe.wait_ge(S["pool_ready"], 3)

            def proj(v, l, t, n0=0, n1=4):
                if n0 == 0:
                    pe.wait_ge(S["wqk_loaded"], l * 16 + 16)
                    if t in (0, TILES):
                        pe.wait_ge(S["xsa_ready"], v + 1 + t // TILES)
                    wait(pe, S["qn_ready"], v * TILES + t)
                c = XPAD + (t % TILES) * P
                for n in range(n0, n1):
                    last = mm(ps[:, n, :], xsa[:, c:c + P], wqk[:, n * 512:(n + 1) * 512], start=True, stop=True)
                    if n % 2 == 1:
                        last.then_inc(S["qk_full"], 1)

            def window_tokens(v, i):
                bank, full = ring_take(v, ("xd", i))
                for j in range(XD_USE):
                    c = (XD_USE * i + j) * W
                    last = tr(bank[:, j * P:(j + 1) * P], xsa[:, c:c + P], ident)
                last.then_inc(full, 1)

            def to_features(v, t, i0, i1):
                r = rot[:, t % 2, :, :].rearrange("p h e -> p (h e)")
                for i in range(i0, i1):
                    if i % 2 == 0:
                        pe.wait_ge(S["rot_ready"], (v * TILES + t) * 2 + i // 2 + 1)
                    bank, full = ring_take(v, ("t", t, i))
                    for j in range(4):
                        c = 4 * i + j
                        last = tr(bank[:, j * P:(j + 1) * P], r[:, c * P:(c + 1) * P], ident)
                    last.then_inc(full, 1)

            def local_scores(v, t, prev, half):
                if half == 0:
                    wait(pe, S["sc_used"], v * TILES + t)
                    ring_emptied(pe, v, ("t", t, 2), ("t", t, 3))
                    if prev and t == 1:
                        pe.wait_ge(S["x1_ready"], v)
                    if prev and t == 3:
                        pe.wait_ge(S["x_done"], v + B)
                    mk = maskb[:, 1 if t == 0 else 0, :].unsqueeze(1).to_broadcast([P, PAIRS, 2 * W])
                    for e in range(2):
                        mm(ps[:, 6 + e, :], identb[:, :], mk, start=True, stop=False, skip_group_check=True)
                for p in range(half * PAIRS // 2, (half + 1) * PAIRS // 2):
                    for i in range(WT):
                        w = t * WT + i
                        for e in range(2):
                            last = mm(ps[W * i:W * i + W, 6 + e, p * 2 * W:(p + 1) * 2 * W],
                                      qT[64 * e:64 * e + 64, t % 2, p, W * i:W * i + W],
                                      kT[64 * e:64 * e + 64, p, W * w:W * w + 2 * W],
                                      start=False, stop=(p == PAIRS - 1), skip_group_check=True)
                if half == 1:
                    last.then_inc(S["sc_full"], 1)

            def probs_to_keys(v, t):
                pe.wait_ge(S["pn_ready"], v * TILES + t + 1)
                for i in range(2):
                    bank, full = ring_take(v, ("p", t, i))
                    for j in range(4):
                        last = tr(bank[:, j * P:(j + 1) * P], pn[:, 4 * i + j, :, :].rearrange("q e k -> q (e k)"), ident)
                    last.then_inc(full, 1)

            def weigh_tokens(v, t, k0=0, k1=4):
                if k0 == 0:
                    ring_emptied(pe, v, ("p", t, 0), ("p", t, 1))
                for k in range(k0, k1):
                    bank, full = ring_take(v, ("y", t, k))
                    wp, e = k // 2, k % 2
                    for i in range(2):
                        wi = 2 * wp + i
                        last = mm(bank[:, i * 256:(i + 1) * 256], xd[64 * e:64 * e + 64, (t % TILES) * WT + wi + 2 * (1 - e), :],
                                  pT[64 * e:64 * e + 64, t % 2, :, W * wi:W * wi + W], start=True, stop=True)
                    last.then_inc(full, 1)

            def attention_out(v, l, e, p0=0, p1=PAIRS):
                if e == 0:
                    pe.wait_ge(S["m_ready"], l * 2 + 2)
                    ring_emptied(pe, v, ("y", -1, 2), ("y", -1, 3))
                    pe.wait_ge(S["sc_used"], UNITS * TILES if isinstance(v, int) and v == UNITS else v * TILES + 1)
                for p in range(p0, p1):
                    last = mm(ps[:, 7, :], mh[:, e, p, :], yT[:, e, p, :], start=(e + p == 0), stop=(e == 1 and p == PAIRS - 1))
                if e == 1 and p1 == PAIRS:
                    last.then_inc(S["attn_full"], 1)

            def to_tokens(v):
                pe.wait_ge(S["xsf_ready"], v)
                bank, full = ring_take(v, ("ln",))
                for t in range(TILES):
                    last = tr(bank[:, t * P:(t + 1) * P], xsf[:, t * P:(t + 1) * P], ident)
                last.then_inc(full, 1)

            def normed_to_features(v):
                pe.wait_ge(S["xn_ready"], v)
                bank, full = ring_take(v, ("xn",))
                for t in range(TILES):
                    last = tr(bank[:, t * P:(t + 1) * P], xn[:, t, :], ident)
                last.then_inc(full, 1)

            def widen(v, l, c):
                if c == 0:
                    pe.wait_ge(S["ffn_loaded"], l * 48 + 48)
                    ring_emptied(pe, v, ("xn",))
                m = P if c < FC - 1 else FREM
                for key, c0 in (("gate", F), ("val", 0)):
                    bank, full = ring_take(v, (key, c))
                    mm(bank[0:m, :], w1_s[:, c0 + c * P:c0 + c * P + m], xnT[:, :], start=True, stop=True).then_inc(full, 1)

            def narrow(v):
                if not (isinstance(v, int) and v == UNITS):
                    pe.wait_ge(S["sc_used"], v * TILES + 3)
                for c in range(FC):
                    m = P if c < FC - 1 else FREM
                    ring_emptied(pe, v, ("val", c))
                    last = mm(ps[:, 6, :], w2_s[0:m, c, :], hT[0:m, c, :], start=(c == 0), stop=(c == FC - 1))
                last.then_inc(S["out_full"], 1)

            def turn(v, l, b, prev, nxt):
                to_m = not (isinstance(b, int) and b == 0)
                if to_m:
                    pe.wait_ge(S["m_ready"], l * 2 + 1)
                proj(v, l, 1, 0, 2)
                to_features(v, 0, 0, 2)
                if to_m:
                    pe.wait_ge(S["m_ready"], l * 2 + 2)
                proj(v, l, 1, 2, 3)
                to_features(v, 0, 2, 4)
                proj(v, l, 1, 3, 4)
                local_scores(v, 0, prev, 0)
                if prev:
                    probs_to_keys(v, -1)
                local_scores(v, 0, prev, 1)
                if prev:
                    weigh_tokens(v, -1)
                for n in range(4):
                    window_tokens(v, n)
                    proj(v, l, 2, n, n + 1)
                window_tokens(v, 4)
                window_tokens(v, 5)
                if prev:
                    attention_out(v, prev[0], 0)
                to_features(v, 1, 0, 2)
                if prev:
                    attention_out(v, prev[0], 1, 0, 2)
                to_features(v, 1, 2, 3)
                if prev:
                    attention_out(v, prev[0], 1, 2, 4)
                if prev:
                    attention_out(v, prev[0], 1, 4, PAIRS)
                to_features(v, 1, 3, 4)
                probs_to_keys(v, 0)
                local_scores(v, 1, prev, 0)
                weigh_tokens(v, 0, 0, 2)
                local_scores(v, 1, prev, 1)
                if prev:
                    to_tokens(v)
                weigh_tokens(v, 0, 2, 4)
                proj(v, l, 3, 0, 2)
                to_features(v, 2, 0, 2)
                proj(v, l, 3, 2, 3)
                to_features(v, 2, 2, 4)
                proj(v, l, 3, 3, 4)
                local_scores(v, 2, prev, 0)
                probs_to_keys(v, 1)
                local_scores(v, 2, prev, 1)
                weigh_tokens(v, 1)
                if prev:
                    normed_to_features(v)
                if nxt:
                    proj(v, nxt[0], TILES, 0, 2)
                if prev:
                    widen(v, prev[0], 0)
                if nxt:
                    proj(v, nxt[0], TILES, 2, 4)
                if prev:
                    widen(v, prev[0], 1)
                to_features(v, 3, 0, 2)
                if prev:
                    widen(v, prev[0], 2)
                to_features(v, 3, 2, 4)
                probs_to_keys(v, 2)
                if prev:
                    narrow(v)
                weigh_tokens(v, 2, 0, 1)
                local_scores(v, 3, prev, 0)
                weigh_tokens(v, 2, 1, 3)
                local_scores(v, 3, prev, 1)
                weigh_tokens(v, 2, 3, 4)

            def build_m(l):
                pe.wait_ge(S["mw_loaded"], l * 32 + 32)
                pe.wait_ge(S["qn_ready"], l * (B * TILES) + (TILES + 1))
                for e in range(2):
                    for p in range(PAIRS):
                        last = mm(ps[:, 2 * e + p // 4, (p % 4) * D:(p % 4 + 1) * D], wv_s[64 * e:64 * e + 64, p, :],
                                  wo_s[64 * e:64 * e + 64, p, :], start=True, stop=True)
                    last.then_inc(S["m_full"], 1)

            def after():
                probs_to_keys(UNITS, -1)
                weigh_tokens(UNITS, -1)
                attention_out(UNITS, L - 1, 0)
                attention_out(UNITS, L - 1, 1)
                to_tokens(UNITS)
                normed_to_features(UNITS)
                for c in range(FC):
                    widen(UNITS, L - 1, c)
                narrow(UNITS)

            proj(0, 0, 0)
            run_turns(pe, turn, build_m, after)
            pe.wait_ge(S["sum_ready"], 1)
            for b in range(B):
                for t in range(TILES):
                    last = tr(ps[:, b, t * P:(t + 1) * P], xT[:, b * T + t * P:b * T + (t + 1) * P], ident)
                last.then_inc(S["fin_full"], 1)

        @block.scalar
        def _(act):
            fn = nc.scalar.activation
            act.wait_ge(S["a_loaded"], 7 * 16)
            with act.Fori(0, B) as b:
                act.wait_ge(S["a_full"], b * TILES)
                act.wait_ge(S["x_done"], B)
                fn(xcur[:, :], xT[:, bass.ts(b, T)], ACT.Copy).then_inc(S["xcur_ready"], 1)
                act.wait_ge(S["lat_full"], b + 1)
                fn(lat[:, :], ps[0:AL, 4, :], ACT.Identity, bias=avs[0:AL, A_BDOWN:A_BDOWN + 1]).then_inc(S["lat_ready"], 1)
                for t in range(TILES):
                    act.wait_ge(S["a_sub"], b * TILES + t + 1)
                    fn(att[:, t, :, :], att[:, t, :, :], ACT.Exp, scale=float(AD) ** -0.5).then_inc(S["a_exp"], 1)
                act.wait_ge(S["ot_full"], b + 1)
                fn(oT[:, :], ps[:, 5, :], ACT.Copy).then_inc(S["ot_ready"], 1)
            act.wait_ge(S["acc_done"], B)
            act.wait_ge(S["pool_ready"], 3)

            def shift(dst, src, signal):
                fn(dst[0:64, :], src[0:64, :], ACT.Copy)
                fn(dst[64:P, 1:T], src[64:P, 0:T - 1], ACT.Copy).then_inc(signal, 1)

            def shift_input(v, b):
                act.wait_ge(S["x_done"], v + 1)
                wait(act, S["qk_full"], v * (TILES * 2))
                shift(xsa[:, XPAD:XPAD + T], xT[:, bass.ts(b, T)], S["xsa_ready"])

            def squares(v, t, s):
                act.wait_ge(S["qk_full"], (v * TILES + t) * 2 + s + 1)
                fn(sq[:, s * H:(s + 1) * H, :].rearrange("p h e -> p (h e)"), ps[:, 2 * s:2 * s + 2, :],
                   ACT.Square).then_inc(S["sq_ready"], 1)

            def window_tokens(v, i):
                bank, free = ring_read(act, v, ("xd", i))
                fn(xd[:, XD_USE * i:XD_USE * (i + 1), :].rearrange("p w d -> p (w d)"), bank[:, 0:XD_USE * P], ACT.Copy).then_inc(free, 1)

            def features(v, t, *quarters):
                for i in quarters:
                    bank, free = ring_read(act, v, ("t", t, i))
                    src = bank.rearrange("p (j q) -> p j q", q=P)
                    p0 = i % 2 * 4
                    dst = qT[:, t % 2, p0:p0 + 4, :] if i < 2 else kT[:, p0:p0 + 4, W + t * P:W + (t + 1) * P]
                    fn(dst, src, ACT.Copy).then_inc(free, 1)

            def exps(v, t):
                act.wait_ge(S["sc_used"], v * TILES + t + 1)
                fn(sm[:, t % 2, :, :], sm[:, t % 2, :, :], ACT.Exp).then_inc(S["p_ready"], 1)

            def probs(v, t):
                for i in range(2):
                    bank, free = ring_read(act, v, ("p", t, i))
                    fn(pT[:, t % 2, 4 * i:4 * i + 4, :], bank.rearrange("p (j q) -> p j q", q=P), ACT.Copy).then_inc(free, 1)

            def weighed(v, t, *quarters):
                for i in quarters or range(4):
                    bank, free = ring_read(act, v, ("y", t, i))
                    c0 = (t % TILES) * P + i // 2 * 2 * W
                    fn(yT[:, i % 2, :, c0:c0 + 2 * W].rearrange("f p (i q) -> f i p q", q=W),
                       bank.rearrange("f (i p q) -> f i p q", p=PAIRS, q=W), ACT.Copy).then_inc(free, 1)

            def shift_middle(v):
                act.wait_ge(S["x1_ready"], v)
                shift(xsf[:, :], x1[:, :], S["xsf_ready"])

            def tokens(v):
                bank, free = ring_read(act, v, ("ln",))
                fn(xn[:, :, :].rearrange("p t d -> p (t d)"), bank, ACT.Copy).then_inc(free, 1)

            def normed(v, l):
                act.wait_ge(S["ffn_loaded"], l * 48 + 48)
                bank, free = ring_read(act, v, ("xn",))
                fn(xnT[:, :], bank, ACT.Identity, scale=fv[:, V_G:V_G + 1], bias=fv[:, V_B:V_B + 1]).then_inc(free, 1)

            def gates(v, c):
                m = P if c < FC - 1 else FREM
                bank, free = ring_read(act, v, ("gate", c))
                fn(gl[0:m, c, :], bank[0:m, :], ACT.Gelu, bias=fv[0:m, V_GATE + c:V_GATE + c + 1]).then_inc(free, 1)

            def turn(v, l, b, prev, nxt):
                features(v, 0, 0, 1)
                squares(v, 1, 0)
                features(v, 0, 2, 3)
                squares(v, 1, 1)
                if prev:
                    probs(v, -1)
                    weighed(v, -1)
                window_tokens(v, 0)
                window_tokens(v, 1)
                window_tokens(v, 2)
                squares(v, 2, 0)
                window_tokens(v, 3)
                window_tokens(v, 4)
                window_tokens(v, 5)
                squares(v, 2, 1)
                exps(v, 0)
                features(v, 1, 0, 1, 2, 3)
                probs(v, 0)
                if prev:
                    shift_middle(v)
                weighed(v, 0, 0, 1)
                if prev:
                    tokens(v)
                weighed(v, 0, 2, 3)
                exps(v, 1)
                features(v, 2, 0, 1)
                squares(v, 3, 0)
                features(v, 2, 2, 3)
                squares(v, 3, 1)
                if nxt:
                    shift_input(v + 1, nxt[1])
                probs(v, 1)
                weighed(v, 1)
                if prev:
                    normed(v, prev[0])
                exps(v, 2)
                if nxt:
                    squares(v, TILES, 0)
                if prev:
                    gates(v, 0)
                if nxt:
                    squares(v, TILES, 1)
                if prev:
                    gates(v, 1)
                features(v, 3, 0, 1)
                if prev:
                    gates(v, 2)
                features(v, 3, 2, 3)
                probs(v, 2)
                weighed(v, 2)
                exps(v, 3)

            def copy_m(l):
                for e in range(2):
                    act.wait_ge(S["m_full"], l * 2 + e + 1)
                    fn(mh[:, e, :, :].rearrange("c p f -> c (p f)"), ps[:, 2 * e:2 * e + 2, :], ACT.Copy).then_inc(S["m_ready"], 1)

            def after():
                probs(UNITS, -1)
                weighed(UNITS, -1)
                shift_middle(UNITS)
                tokens(UNITS)
                normed(UNITS, L - 1)
                for c in range(FC):
                    gates(UNITS, c)

            shift_input(0, 0)
            squares(0, 0, 0)
            squares(0, 0, 1)
            run_turns(act, turn, copy_m, after)

        @block.vector
        def _(dve):
            v = nc.vector

            class Steps:
                def __init__(self, sem_, base):
                    self.sem, self.base, self.n = sem_, base, 0

                def done(self, ins):
                    self.n += 1
                    ins.then_inc(self.sem, 1)
                    dve.wait_ge(self.sem, self.base + self.n)

            def rsqrt(step, src, c0, c1):
                y, t = ny[:, c0:c1], nt[:, c0:c1]
                step.done(v.tensor_scalar(t.bitcast(I32), src.bitcast(I32), 1, None, ALU.logical_shift_right))
                step.done(v.tensor_scalar(y.bitcast(I32), t.bitcast(I32), -1.0, float(RSQRT_MAGIC), ALU.mult, ALU.add))
                for _ in range(3):
                    step.done(v.scalar_tensor_tensor(out=t, in0=y, scalar=-0.5, in1=y, op0=ALU.mult, op1=ALU.mult))
                    step.done(v.tensor_tensor(t, t, src, ALU.mult))
                    step.done(v.scalar_tensor_tensor(out=y, in0=t, scalar=1.5, in1=y, op0=ALU.add, op1=ALU.mult))

            def token_stats(step, source, n, variances):
                for i in range(n):
                    last = v.bn_stats(st6[:, i, :], source(i))
                step.done(last)
                v.memset(spare[:, 0:1], 0.0)
                for i in range(n):
                    last = v.bn_aggr(mv[:, i, :], st6[:, i, :])
                step.done(last)
                step.done(v.tensor_scalar(variances, mv[:, 0:n, 1], EPS, None, ALU.add))

            dve.wait_ge(S["x_loaded"], 16)
            step = Steps(S["pro_chain"], 0)
            token_stats(step, lambda i: xtok[:, i, :], B * TILES, ss0[:, :])
            rsqrt(step, ss0[:, :], 0, B * TILES)
            for i in range(B * TILES):
                ins = v.tensor_scalar(xn0[:, i, :], xtok[:, i, :], mv[:, i, 0:1], ny[:, i:i + 1], ALU.subtract, ALU.mult)
                if i % TILES == TILES - 1:
                    ins.then_inc(S["xn0_ready"], 1)
            dve.wait_ge(S["const_loaded"], 16)
            v.tensor_copy(identb[:, :], ident).then_inc(S["casts"], 1)
            v.tensor_copy(maskb[:, 0, :], consts[:, C_MASK:C_MASK + 2 * W]).then_inc(S["casts"], 1)
            v.tensor_copy(maskb[:, 1, :], consts[:, C_MASK0:C_MASK0 + 2 * W]).then_inc(S["casts"], 1)
            for b in range(B):
                dve.wait_ge(S["pro_full"], b + 1)
                v.tensor_copy(xT[:, b * T:(b + 1) * T], ps[:, b, :]).then_inc(S["x_done"], 1)

            dve.wait_ge(S["a_loaded"], 7 * 16)
            with dve.Fori(0, B) as b:
                step = Steps(S["a_chain"], b * A_STEPS)

                def rotate_qk(t):
                    dve.wait_ge(S["a_o"], b * TILES)
                    dve.wait_ge(S["a_full"], b * TILES + t + 1)
                    step.done(v.tensor_tensor(qkv[:, t, :], ps[:, t, 0:3 * P], abb[:, :], ALU.add))
                    def heads(a):
                        return a[:, t, 0:2 * P].rearrange("p (h d) -> p h d", d=AD)
                    def table(i, o, n):
                        return atb[:, i, t, o:o + n].unsqueeze(1).to_broadcast([P, 2 * AH, n])
                    v.tensor_tensor(heads(rqk), heads(qkv), table(0, 0, AD), ALU.mult)
                    n = AD // 2
                    for o, i in ((0, n), (n, 0)):
                        last = v.tensor_tensor(heads(rsin)[:, :, o:o + n], heads(qkv)[:, :, i:i + n], table(1, o, n), ALU.mult)
                    step.done(last)
                    v.tensor_tensor(rqk[:, t, :], rqk[:, t, :], rsin[:, t, :], ALU.add).then_inc(S["a_rot"], 1)

                def reduce_qk(t):
                    dve.wait_ge(S["a_qk"], b * TILES + t + 1)
                    step.done(v.tensor_reduce(att[:, t, :, :].rearrange("p h g -> p (h g)"), prodq[:, t % 2, :, :], AXX, ALU.add))
                    step.done(v.tensor_reduce(am[:, t, 0, :], att[:, t, :, :], AXX, ALU.max, negate=True))
                    v.tensor_tensor(att[:, t, :, :], att[:, t, :, :], am[:, t, 0, :].unsqueeze(2).to_broadcast([P, AH, AH]),
                                    ALU.add).then_inc(S["a_sub"], 1)

                def weigh_v(t):
                    dve.wait_ge(S["a_exp"], b * TILES + t + 1)
                    if t >= 2:
                        dve.wait_ge(S["a_o"], b * TILES + t - 1)
                    v.tensor_tensor(*pv_operands(t, 0), ALU.mult).then_inc(S["a_pvd"], 1)
                    step.done(v.tensor_reduce(am[:, t, 1, :], att[:, t, :, :], AXX, ALU.add))
                    v.reciprocal(am[:, t, 2, :], am[:, t, 1, :])
                    dve.wait_ge(S["a_pvd"], b * TILES + t + 1)
                    dve.wait_ge(S["a_pvp"], b * TILES + t + 1)
                    v.tensor_reduce(oraw[:, t, :], prodv[:, t % 2, :, :], AXX, ALU.add).then_inc(S["a_sum"], 1)
                    dve.wait_ge(S["a_sum"], b * TILES + t + 1)
                    v.tensor_tensor(on[:, t, :].rearrange("p (h d) -> p h d", d=AD), oraw[:, t, :].rearrange("p (h d) -> p h d", d=AD),
                                    am[:, t, 2, :].unsqueeze(2).to_broadcast([P, AH, AD]), ALU.mult).then_inc(S["a_o"], 1)

                for t in range(TILES + 2):
                    if t < TILES:
                        rotate_qk(t)
                    if 1 <= t <= TILES:
                        reduce_qk(t - 1)
                    if t >= 2:
                        weigh_v(t - 2)
                dve.wait_ge(S["at_full"], b + 1)
                v.tensor_scalar(accT[:, bass.ts(b, T)], ps[:, 6, :], avs[:, A_BOUT:A_BOUT + 1], None, ALU.add).then_inc(S["acc_done"], 1)
                assert step.n == A_STEPS, step.n

            v_ = nc.vector

            def squared_norms(v, t):
                for s in range(2):
                    dve.wait_ge(S["sq_ready"], (v * TILES + t) * 2 + s + 1)
                    last = v_.tensor_reduce(ss[:, s * H:(s + 1) * H], sq[:, s * H:(s + 1) * H, :], AXX, ALU.add)
                last.then_inc(S["norm_chain"], 1)

            def norms(v, t):
                step = Steps(S["norm_chain"], (v * TILES + t) * TILE_STEPS + 1)
                dve.wait_ge(S["norm_chain"], (v * TILES + t) * TILE_STEPS + 1)
                step.done(v_.tensor_scalar(ss[:, 0:2 * H], ss[:, 0:2 * H], 1e-24, None, ALU.max))
                rsqrt(step, ss[:, 0:2 * H], 0, 2 * H)
                assert step.n == TILE_STEPS - 1

            def normalised(v, t):
                for s in range(2):
                    last = v_.tensor_tensor(qn[:, t % 2, s * H:(s + 1) * H, :],
                                            ps[:, 2 * s:2 * s + 2, :].rearrange("p k (h e) -> p (k h) e", e=E),
                                            ny[:, s * H:(s + 1) * H].unsqueeze(2).to_broadcast([P, H, E]), ALU.mult)
                last.then_inc(S["qn_ready"], 1)

            def add_sines(v, t, s):
                n, heads = (v * TILES + t) * 2 + s + 1, slice(s * H, (s + 1) * H)
                dve.wait_ge(S["ms_ready"], n)
                dve.wait_ge(S["rotc_done"], n)
                v_.tensor_tensor(rot[:, t % 2, heads, :], rot[:, t % 2, heads, :], ms[:, heads, :], ALU.add).then_inc(S["rot_ready"], 1)

            def normalise(v, t):
                squared_norms(v, t)
                norms(v, t)
                normalised(v, t)

            def sine_terms(v, l, t):
                dve.wait_ge(S["qn_ready"], v * TILES + t + 1)
                dve.wait_ge(S["tab_ready"], l * 4 + 4)
                wait(dve, S["rot_ready"], (v * TILES + t) * 2)
                for s in range(2):
                    for half in range(2):
                        o, i = half * E // 2, (1 - half) * E // 2
                        last = v_.tensor_tensor(ms[:, s * H:(s + 1) * H, o:o + E // 2],
                                                qn[:, t % 2, s * H:(s + 1) * H, i:i + E // 2],
                                                tab[:, 2 * s + 1, t % TILES, o:o + E // 2].unsqueeze(1).to_broadcast([P, H, E // 2]), ALU.mult)
                    last.then_inc(S["ms_ready"], 1)

            def shift_scores(v, t):
                step = Steps(S["soft_chain"], (v * TILES + t) * SOFT_STEPS)
                wait(dve, S["sc_used"], v * TILES + t)
                dve.wait_ge(S["sc_full"], v * TILES + t + 1)
                sc = ps[:, 6:8, :].rearrange("p e (h k) -> p (e h) k", k=2 * W)
                step.done(v_.tensor_reduce(negm[:, :], sc, AXX, ALU.max, negate=True))
                v_.tensor_tensor(sm[:, t % 2, :, :], sc, negm[:, :].unsqueeze(2).to_broadcast([P, H, 2 * W]),
                                 ALU.add).then_inc(S["sc_used"], 1)

            def sum_probs(v, t):
                step = Steps(S["soft_chain"], (v * TILES + t) * SOFT_STEPS + 1)
                wait(dve, S["rinv_ready"], v * TILES + t)
                dve.wait_ge(S["p_ready"], v * TILES + t + 1)
                step.done(v_.tensor_reduce(psum_[:, :], sm[:, t % 2, :, :], AXX, ALU.add))
                v_.reciprocal(rinv[:, t % 2, :], psum_[:, :]).then_inc(S["rinv_ready"], 1)

            def middle(v, b):
                dve.wait_ge(S["attn_full"], v)
                dve.wait_ge(S["x_done"], v - 1 + B)
                v_.tensor_tensor(x1[:, :], ps[:, 7, :], xT[:, bass.ts(b, T)], ALU.add).then_inc(S["x1_ready"], 1)

            def stats(v):
                step = Steps(S["ln_chain"], (v - 1) * LN_STEPS)
                ring_emptied(dve, v, ("ln",))
                token_stats(step, lambda i: xn[:, i, :], TILES, ss[:, 2 * H:2 * H + TILES])

            def norm_tokens(v):
                step = Steps(S["ln_chain"], (v - 1) * LN_STEPS + 3)
                rsqrt(step, ss[:, 2 * H:2 * H + TILES], 2 * H, 2 * H + TILES)
                for i in range(TILES):
                    last = v_.tensor_scalar(xn[:, i, :], xn[:, i, :], mv[:, i, 0:1], ny[:, 2 * H + i:2 * H + i + 1], ALU.subtract, ALU.mult)
                last.then_inc(S["xn_ready"], 1)

            def gated(v, c):
                m = P if c < FC - 1 else FREM
                ring_emptied(dve, v, ("gate", c))
                bank, free = ring_read(dve, v, ("val", c))
                v_.scalar_tensor_tensor(out=hT[0:m, c, :], in0=bank[0:m, :], scalar=fv[0:m, V_A + c:V_A + c + 1],
                                        in1=gl[0:m, c, :], op0=ALU.add, op1=ALU.mult).then_inc(free, 1)

            def finish(v, b):
                dve.wait_ge(S["out_full"], v)
                dve.wait_ge(S["x1_ready"], v)
                v_.scalar_tensor_tensor(out=xT[:, bass.ts(b, T)], in0=ps[:, 6, :], scalar=fv[:, V_B2:V_B2 + 1], in1=x1[:, :],
                                        op0=ALU.add, op1=ALU.add).then_inc(S["x_done"], 1)

            def turn(v, l, b, prev, nxt):
                normalise(v, 1)
                shift_scores(v, 0)
                sine_terms(v, l, 1)
                add_sines(v, 1, 0)
                sum_probs(v, 0)
                add_sines(v, 1, 1)
                normalise(v, 2)
                sine_terms(v, l, 2)
                if prev:
                    middle(v, prev[1])
                add_sines(v, 2, 0)
                add_sines(v, 2, 1)
                shift_scores(v, 1)
                if prev:
                    stats(v)
                sum_probs(v, 1)
                if prev:
                    norm_tokens(v)
                normalise(v, 3)
                shift_scores(v, 2)
                sine_terms(v, l, 3)
                if prev:
                    gated(v, 0)
                add_sines(v, 3, 0)
                sum_probs(v, 2)
                if prev:
                    gated(v, 1)
                add_sines(v, 3, 1)
                if nxt:
                    squared_norms(v, TILES)
                if prev:
                    gated(v, 2)
                if nxt:
                    norms(v, TILES)
                    normalised(v, TILES)
                if prev:
                    finish(v, prev[1])
                if nxt:
                    sine_terms(v, nxt[0], TILES)
                    add_sines(v, TILES, 0)
                    add_sines(v, TILES, 1)
                shift_scores(v, 3)
                sum_probs(v, 3)

            def after():
                middle(UNITS, B - 1)
                stats(UNITS)
                norm_tokens(UNITS)
                for c in range(FC):
                    gated(UNITS, c)
                finish(UNITS, B - 1)

            normalise(0, 0)
            sine_terms(0, 0, 0)
            add_sines(0, 0, 0)
            add_sines(0, 0, 1)
            run_turns(dve, turn, lambda l: None, after)

            dve.wait_ge(S["x_done"], B + L * B)
            v.tensor_tensor(xT[:, :], xT[:, :], accT[:, :], ALU.add).then_inc(S["sum_ready"], 1)
            for b in range(B):
                dve.wait_ge(S["fin_full"], b + 1)
                dve.wait_ge(S["x_loaded"], 32)
                tok = ytok[:, b * TILES:(b + 1) * TILES, :].rearrange("p n d -> p (n d)")
                v.tensor_tensor(tok, ps[:, b, :], tok, ALU.add).then_inc(S["y_ready"], 1)

        @block.gpsimd
        def _(pool):
            g = nc.gpsimd
            with pool.Fori(0, B) as b:
                for t in range(TILES + 2):
                    if t < TILES:
                        pool.wait_ge(S["a_rot"], b * TILES + t + 1)
                        pool.wait_ge(S["a_sub"], b * TILES + max(0, t - 1))
                        q = rqk[:, t, 0:P].rearrange("p (h d) -> p h d", d=AD).unsqueeze(2).to_broadcast([P, AH, AH, AD])
                        k = rqk[:, t, P:2 * P].rearrange("p (g d) -> p g d", d=AD).unsqueeze(1).to_broadcast([P, AH, AH, AD])
                        g.tensor_tensor(prodq[:, t % 2, :, :].rearrange("p (h g) d -> p h g d", g=AH), q, k,
                                        ALU.mult).then_inc(S["a_qk"], 1)
                    if t >= 2:
                        pool.wait_ge(S["a_exp"], b * TILES + t - 1)
                        pool.wait_ge(S["a_o"], b * TILES + max(0, t - 3))
                        g.tensor_tensor(*pv_operands(t - 2, 1), ALU.mult).then_inc(S["a_pvp"], 1)
            pool.wait_ge(S["acc_done"], B)
            g.memset(xsa[:, :], 0.0).then_inc(S["pool_ready"], 1)
            pool.wait_ge(S["pool_ready"], 1)
            g.memset(xsf[:, :], 0.0).then_inc(S["pool_ready"], 1)
            pool.wait_ge(S["pool_ready"], 2)
            g.memset(kT[:, :, 0:W], 0.0).then_inc(S["pool_ready"], 1)
            pool.wait_ge(S["pool_ready"], 3)
            pool.wait_ge(S["tabb_loaded"], 16)

            def tables(l):
                pool.wait_ge(S["qkv_loaded"], l * 16 + 16)
                wait(pool, S["ms_ready"], l * (B * TILES * 2))
                wait(pool, S["rotc_done"], l * (B * TILES * 2))
                for k in range(4):
                    g.tensor_tensor(tab[:, k, :, :], tabb[:, k, :, :], qkvec[:, k, :].unsqueeze(1).to_broadcast([P, TILES, E]),
                                    ALU.mult).then_inc(S["tab_ready"], 1)

            def rotate(v, l, t):
                pool.wait_ge(S["tab_ready"], l * 4 + 4)
                pool.wait_ge(S["qn_ready"], v * TILES + t + 1)
                for s in range(2):
                    heads = slice(s * H, (s + 1) * H)
                    g.tensor_tensor(rot[:, t % 2, heads, :], qn[:, t % 2, heads, :],
                                    tab[:, 2 * s, t % TILES, :].unsqueeze(1).to_broadcast([P, H, E]), ALU.mult).then_inc(S["rotc_done"], 1)

            def divide(v, t, prev):
                pool.wait_ge(S["rinv_ready"], v * TILES + t + 1)
                if t or prev:
                    ring_emptied(pool, v, ("p", t - 1, 1))
                g.tensor_tensor(pn[:, :, :, :].rearrange("q p e k -> q e p k"),
                                sm[:, t % 2, :, :].rearrange("q (e p) k -> q e p k", e=2),
                                rinv[:, t % 2, :].rearrange("q (e p) -> q e p", e=2).unsqueeze(3)
                                .to_broadcast([P, 2, PAIRS, 2 * W]), ALU.mult).then_inc(S["pn_ready"], 1)

            def turn(v, l, b, prev, nxt):
                for t in range(TILES):
                    if t < TILES - 1:
                        rotate(v, l, t + 1)
                    elif nxt:
                        if isinstance(b, int) and b == B - 1:
                            tables(nxt[0])
                        rotate(v, nxt[0], TILES)
                    divide(v, t, prev)

            tables(0)
            rotate(0, 0, 0)
            run_turns(pool, turn, lambda l: None, lambda: None)


def constants():
    import numpy as np
    f = np.float32
    cst = np.zeros((P, C_END), f)
    cst[:, C_ID:C_ID + P] = np.eye(P)
    i, j = np.arange(P)[:, None] % W, np.arange(2 * W)[None]
    seen = (i <= j) & (j <= i + W)
    cst[:, C_MASK:C_MASK + 2 * W] = np.where(seen, 0, NEG)
    cst[:, C_MASK0:C_MASK0 + 2 * W] = np.where(seen & ((np.arange(P)[:, None] >= W) | (j >= W)), 0, NEG)
    t = np.arange(T, dtype=f)
    inv = (f(1) / f(10000) ** (np.arange(0, AD, 2, dtype=f) / f(AD))).astype(f)
    fr = t[:, None] * inv[None]
    c, s = np.cos(fr), np.sin(fr)
    tiled = lambda a: a.reshape(TILES, P, -1).transpose(1, 0, 2)
    atab = np.stack([tiled(np.concatenate(a, 1)) for a in ((c, c), (-s, s))], 1).astype(f)
    half = np.arange(0, E, 2, dtype=f)
    inv = (f(1) / f(10000) ** (half / f(E))).astype(f)
    fr = t[:, None] * inv[None]
    base = ((half + f(0.4 * E)) / f(1.4 * E)).astype(f)
    sc = base[None] ** ((t - T // 2) / f(W // 2))[:, None]
    c, s = np.cos(fr), np.sin(fr)
    both = lambda a, b: np.concatenate([a, b], 1)
    tabs = [both(8 * c * sc, 8 * c * sc), both(-8 * s * sc, 8 * s * sc), both(c / sc, c / sc), both(-s / sc, s / sc)]
    ftab = np.stack([tiled(a) for a in tabs], 1).astype(f)
    return cst, atab, ftab


def kernel(**inputs):
    import numpy as np
    import concourse.bacc as bacc
    from concourse.bass_utils import run_bass_kernel_spmd

    a = {k[3:]: np.asarray(v) for k, v in inputs.items()}
    swap64 = (np.arange(E) + E // 2) % E

    def column(*vs):
        return np.stack([np.concatenate([v, np.zeros(P - len(v), v.dtype)]) for v in vs], 1)

    wup, bup = (a[k].reshape(-1, AH, 2, AD) for k in ("attn_Wup", "attn_bup"))
    wup, bup = (np.concatenate([z[:, :, 0].reshape(-1, P), z[:, :, 1].transpose(0, 2, 1).reshape(-1, P)], 1) for z in (wup, bup))
    w2 = np.zeros((L, FC * P, D), a["ffn_W2"].dtype)
    w2[:, 0:F] = a["ffn_W2"]
    cuts = lambda v: [v[i:i + P] for i in range(0, F, P)]
    qs, ks = a["ffn_q_scale"], a["ffn_k_scale"]
    cst, atab, ftab = constants()
    arrays = {
        "x": a["attn_x"],
        "avec": column(a["attn_bout"], a["attn_bdown"]),
        "abias": np.concatenate([a["attn_bq"], bup[0]]),
        "wq": a["attn_Wq"],
        "wdown": a["attn_Wdown"],
        "wup": wup,
        "wout": a["attn_Wout"],
        "wqkv": a["ffn_Wqkv"],
        "wvt": a["ffn_Wqkv"][:, :, 2 * INNER:].transpose(0, 2, 1),
        "wo": a["ffn_Wo"],
        "w1": a["ffn_W1"],
        "w2": w2,
        "fvec": np.stack([column(a["ffn_ln_g"][i], a["ffn_ln_b"][i], *cuts(a["ffn_b1"][i, 0:F]), *cuts(a["ffn_b1"][i, F:]),
                                 a["ffn_b2"][i]) for i in range(L)]),
        "qks": np.stack([qs, qs[:, swap64], ks, ks[:, swap64]], 1),
        "cst": cst, "atab": atab, "ftab": ftab,
    }
    nc = bacc.Bacc("TRN2", target_bir_lowering=False, num_devices=1)
    arrays = {f"in_{k}": np.ascontiguousarray(v) for k, v in arrays.items()}
    args = [nc.dram_tensor(k, v.shape, mybir.dt.from_np(v.dtype), kind="ExternalInput").ap() for k, v in arrays.items()]
    y = nc.dram_tensor("out_0", (B, T, D), F32, kind="ExternalOutput").ap()
    program(nc, *args, y)
    r = run_bass_kernel_spmd(nc, [arrays], core_ids=[0])
    return r.results[0]["out_0"]
```

```python
from contextlib import ExitStack

import concourse.bass as bass
from concourse import mybir

F32 = mybir.dt.float32
BF16 = mybir.dt.bfloat16
I32 = mybir.dt.int32
ALU = mybir.AluOpType
ACT = mybir.ActivationFunctionType
AXX = mybir.AxisListType.X

P = 128
B, T, D = 4, 512, 128
TILES = T // P
AH, AD, AL = 16, 8, 32
L, H, E, W = 6, 16, 64, 32
PAIRS = H // 2
WT = P // W
INNER = H * E
F = int(D * 4 * 2 / 3)
FC = -(-F // P)
FREM = F - (FC - 1) * P
NEG = -1e30
EPS = 1e-5
RSQRT_MAGIC = 0x5F3759DF
C_ID, C_MASK, C_MASK0, C_END = 0, P, P + 2 * W, P + 4 * W
V_G, V_B, V_A, V_GATE, V_B2, V_END = 0, 1, 2, 2 + FC, 2 + 2 * FC, 3 + 2 * FC
A_BOUT, A_BDOWN, A_END = 0, 1, 2

XD_SLOTS = TILES * WT + 2
XD_USE = 3
XD_USES = XD_SLOTS // XD_USE
XPAD = 3 * W
AFTER = [("p", -1, i) for i in range(2)] + [("y", -1, i) for i in range(4)]
FFN = [(k, c) for c in range(1, FC) for k in ("gate", "val")]
RING = (
    [("t", 0, i) for i in range(4)] + AFTER
    + [("xd", i) for i in range(XD_USES)]
    + [("t", 1, i) for i in range(4)] + [("p", 0, i) for i in range(2)] + [("y", 0, 0), ("y", 0, 1), ("ln",), ("y", 0, 2), ("y", 0, 3)]
    + [("t", 2, i) for i in range(4)] + [("p", 1, i) for i in range(2)] + [("y", 1, i) for i in range(4)] + [("xn",)]
    + FFN[0:2] + [("t", 3, 0), ("t", 3, 1)] + FFN[2:] + [("t", 3, 2), ("t", 3, 3)]
    + [("p", 2, i) for i in range(2)] + [("y", 2, i) for i in range(4)]
)
RING_PREV = AFTER + [("ln",), ("xn",)] + FFN
RING_HALF = len(RING) // 2
assert len(RING) % 2 == 0
UNITS = L * B
NORM_STEPS = 11
LN_STEPS = 3 + NORM_STEPS
TILE_STEPS = 2 + NORM_STEPS
SOFT_STEPS = 2
A_STEPS = 1 + 2 + 2


def program(nc, x, avec, abias, wq, wdown, wup, wout, wqkv, wvt, wo, w1, w2, fvec, qks, cst, atab, ftab, out):
    ctx = ExitStack()
    with ctx:
        def sbuf(name, shape, dt=F32, where=ctx):
            return where.enter_context(nc.sbuf_tensor(name, shape, dt))

        def sem(name):
            return ctx.enter_context(nc.semaphore(name))

        ps = ctx.enter_context(nc.psum_tensor("banks", [P, 8, 512], F32))
        xT = sbuf("xT", [P, B * T])
        accT = sbuf("accT", [P, B * T])
        consts = sbuf("consts", [P, C_END])
        ident = consts[:, C_ID:C_ID + P]
        identb = sbuf("identb", [P, P], BF16)
        maskb = sbuf("maskb", [P, 2, 2 * W], BF16)
        st6 = sbuf("st6", [P, B * TILES, 6])
        mv = sbuf("mv", [P, B * TILES, 2])
        spare = sbuf("spare", [P, 4])
        ss0 = sbuf("ss0", [P, B * TILES])
        ny = sbuf("ny", [P, 2 * H + TILES])
        nt = sbuf("nt", [P, 2 * H + TILES])

        atb = sbuf("attn_tables", [P, 2, TILES, AD])
        avs = sbuf("avs", [P, A_END])
        abb = sbuf("attn_bias_rows", [P, 3 * P])
        wq_s = sbuf("wq_s", [P, P])
        wdn_s = sbuf("wdn_s", [P, AL])
        wup_s = sbuf("wup_s", [AL, 2 * P])
        wout_s = sbuf("wout_s", [P, D])
        xcur = sbuf("xcur", [P, P])
        lat = sbuf("lat", [AL, P])
        qkv = sbuf("qkv", [P, 3 * P])
        rsin = sbuf("rsin", [P, 2 * P])
        rqk = sbuf("rqk", [P, 2 * P])
        prod = sbuf("prod", [P, AH * AH * AD])
        att = sbuf("att", [P, AH, AH])
        am = sbuf("am", [P, 3, AH])
        oraw = sbuf("oraw", [P, P])
        on = sbuf("on", [P, P])
        oT = sbuf("oT", [P, P])

        aux = ExitStack()
        xn0 = sbuf("xn0", [P, B * TILES, D], F32, aux)
        xtok = sbuf("xtok", [P, B * TILES, D], F32, aux)
        aux.close()

        wqk = sbuf("wqk", [P, 2 * INNER])
        wv_s = sbuf("wv_s", [P, PAIRS, D])
        wo_s = sbuf("wo_s", [P, PAIRS, D])
        mh = sbuf("mh", [P, 2, PAIRS, D])
        w1_s = sbuf("w1_s", [P, 2 * F])
        w2_s = sbuf("w2_s", [P, FC, D])
        fv = sbuf("fv", [P, V_END])
        qkvec = sbuf("qk_vec", [P, 4, E])
        tabb = sbuf("tab_base", [P, 4, TILES, E])
        tab = sbuf("tab", [P, 4, TILES, E])
        xsa = sbuf("xsa", [P, XPAD + T + 2 * W])
        xsf = sbuf("xsf", [P, T])
        xd = sbuf("xd", [P, XD_SLOTS, D])
        sq = sbuf("sq", [P, 2 * H, E])
        qn = sbuf("qn", [P, 2 * H, E])
        rot = sbuf("rot", [P, 2, 2 * H, E])
        ms = sbuf("ms", [P, 2 * H, E])
        qT = sbuf("qT", [P, 2, PAIRS, P])
        kT = sbuf("kT", [P, PAIRS, W + T])
        ss = sbuf("ss", [P, 2 * H + TILES])
        negm = sbuf("negm", [P, 2 * PAIRS])
        psum_ = sbuf("prob_sum", [P, 2 * PAIRS])
        rinv = sbuf("rinv", [P, 2, 2 * PAIRS])
        sm = sbuf("sm", [P, 2 * PAIRS, 2 * W])
        pn = sbuf("pn", [P, PAIRS, 2, 2 * W])
        pT = sbuf("pT", [P, PAIRS, P])
        yT = sbuf("yT", [P, 2, PAIRS, T])
        x1 = sbuf("x1", [P, T])
        xn = sbuf("xn", [P, TILES, D])
        xnT = xn[:, :, :].rearrange("p n d -> p (n d)")
        ytok = rot[:, 0, :, :].rearrange("p h e -> p (h e)").rearrange("p (n d) -> p n d", d=D)
        gl = sbuf("gl", [P, FC, T])
        hT = gl

        names = """x_loaded const_loaded a_loaded pool_ready casts pro_chain xn0_ready pro_full x_done
        xcur_ready lat_full lat_ready a_full a_bias a_chain a_rot a_qk a_sub a_exp a_pv a_o ot_full ot_ready at_full acc_done
        mw_loaded qkv_loaded wqk_loaded ffn_loaded tabb_loaded m_full m_ready tab_ready
        xsa_ready xsf_ready qk_full sq_ready qn_ready xn_ready rotc_done ms_ready rot_ready
        gate0_full gate0_read val0_full val0_read sc_full sc_used p_ready rinv_ready pn_ready attn_full x1_ready out_full
        norm_chain soft_chain ln_chain sum_ready fin_full y_ready y_stored""".split()
        S = {n: sem(n) for n in names}
        ring_full = [sem("ring_full0"), sem("ring_full1")]
        ring_free = [sem("ring_free0"), sem("ring_free1")]

        def wait(eng, semaphore, count):
            if not (isinstance(count, int) and count <= 0):
                eng.wait_ge(semaphore, count)

        def ring_use(v, key):
            i = RING.index(key)
            r = i % 2
            if isinstance(v, int) and v == 0:
                return r, sum(k not in RING_PREV for k in RING[r:i:2])
            skipped = sum(k in RING_PREV for k in RING[r::2])
            if isinstance(v, int) and v == UNITS:
                return r, v * RING_HALF - skipped + sum(k in RING_PREV for k in RING[r:i:2])
            return r, v * RING_HALF + (i // 2 - skipped)

        def ring_take(v, key):
            r, n = ring_use(v, key)
            wait(nc.tensor, ring_free[r], n)
            return ps[:, 4 + r, :], ring_full[r]

        def ring_read(eng, v, key):
            r, n = ring_use(v, key)
            eng.wait_ge(ring_full[r], n + 1)
            return ps[:, 4 + r, :], ring_free[r]

        def ring_emptied(eng, v, *keys):
            for key in keys:
                r, n = ring_use(v, key)
                eng.wait_ge(ring_free[r], n + 1)

        def ffn_take(v, key, c):
            if c:
                return ring_take(v, (key, c))
            if key == "gate" and not (isinstance(v, int) and v == UNITS):
                nc.tensor.wait_ge(S["sc_used"], v * TILES + 3)
            return ps[:, 7 if key == "gate" else 6, :], S[key + "0_full"]

        def ffn_read(eng, v, key, c):
            if c:
                return ring_read(eng, v, (key, c))
            eng.wait_ge(S[key + "0_full"], v)
            return ps[:, 7 if key == "gate" else 6, :], S[key + "0_read"]

        def ffn_done(eng, v, key, c):
            if c:
                ring_emptied(eng, v, (key, c))
            else:
                eng.wait_ge(S[key + "0_read"], v)

        def run_turns(eng, turn, first_layer_use, after):
            def rest(l, attention):
                first_layer_use(l)
                with eng.Fori(1, B - 1) as b:
                    turn(l * B + b, l, b, (l, b - 1), (l, b + 1), b - 1 if attention else None)
                last, at = l == L - 1 if isinstance(l, int) else False, B - 2 if attention else None
                turn(l * B + (B - 1), l, B - 1, (l, B - 2), None if last else (l + 1, 0), at)
                if not last:
                    turn(l * B + B, l + 1, 0, (l, B - 1), (l + 1, 1), B - 1 if attention else None)
            turn(0, 0, 0, None, (0, 1), None)
            with eng.Fori(0, B) as l:
                rest(l, True)
            for l in range(B, L):
                rest(l, False)
            after()

        assert B == TILES
        block = ctx.enter_context(nc.Block())

        @block.sync
        def _(sp):
            sp.dma_start(xtok[:, :, :], x.rearrange("b (n p) d -> p (b n) d", p=P)).then_inc(S["x_loaded"], 16)
            sp.dma_start(consts[:, :], cst).then_inc(S["const_loaded"], 16)
            for dst, src in ((avs[:, :], avec), (wq_s[:, :], wq), (wdn_s[:, :], wdown), (wup_s[:, :], wup),
                             (abb[:, :], abias.rearrange("(a n) -> a n", a=1).to_broadcast([P, 3 * P])),
                             (atb[:, :, :, :], atab), (wout_s[:, :], wout)):
                sp.dma_start(dst, src).then_inc(S["a_loaded"], 16)
            sp.wait_ge(S["x_done"], B)
            sp.dma_start(tabb[:, :, :, :], ftab).then_inc(S["tabb_loaded"], 16)

            def load_layer(l):
                layer = lambda a: a[bass.ds(l, 1)]
                wait(sp, S["tab_ready"], l * 4)
                sp.dma_start(qkvec[:, :, :], layer(qks).to_broadcast([P, 4, E])).then_inc(S["qkv_loaded"], 16)
                wait(sp, S["qk_full"], l * (B * TILES * 2))
                sp.dma_start(wqk[:, :], wqkv[bass.ds(l, 1), :, 0:2 * INNER].rearrange("l k n -> k (l n)")).then_inc(S["wqk_loaded"], 16)
                wait(sp, S["m_ready"], l * 2)
                sp.dma_start(wv_s[:, :, :], layer(wvt).rearrange("l (p k) c -> k (l p) c", k=P)).then_inc(S["mw_loaded"], 16)
                sp.dma_start(wo_s[:, :, :], layer(wo).rearrange("l (p k) c -> k (l p) c", k=P)).then_inc(S["mw_loaded"], 16)
                sp.wait_ge(S["x_done"], l * B + B)
                sp.dma_start(w1_s[:, :], layer(w1).rearrange("l k n -> k (l n)")).then_inc(S["ffn_loaded"], 16)
                sp.dma_start(w2_s[:, :, :], layer(w2).rearrange("l (c k) n -> k (l c) n", k=P)).then_inc(S["ffn_loaded"], 16)
                sp.dma_start(fv[:, :], layer(fvec).rearrange("l k n -> k (l n)")).then_inc(S["ffn_loaded"], 16)

            load_layer(0)
            with sp.Fori(1, L) as l:
                load_layer(l)
            sp.wait_ge(S["x_done"], B + L * B)
            sp.dma_start(ytok, x.rearrange("b (n p) d -> p (b n) d", p=P)).then_inc(S["x_loaded"], 16)
            for b in range(B):
                sp.wait_ge(S["y_ready"], b + 1)
                sp.dma_start(out[b].rearrange("(n p) d -> p n d", p=P), ytok[:, b * TILES:(b + 1) * TILES, :]).then_inc(S["y_stored"], 16)
            sp.wait_ge(S["y_stored"], 16 * B)

        @block.tensor
        def _(pe):
            mm, tr = nc.tensor.matmul, nc.tensor.transpose
            pe.wait_ge(S["const_loaded"], 16)
            for b in range(B):
                pe.wait_ge(S["xn0_ready"], b + 1)
                for t in range(TILES):
                    last = tr(ps[:, b, t * P:(t + 1) * P], xn0[:, b * TILES + t, :], ident)
                last.then_inc(S["pro_full"], 1)
            pe.wait_ge(S["x_done"], B)
            pe.wait_ge(S["a_loaded"], 7 * 16)

            def latent(v):
                pe.wait_ge(S["xcur_ready"], v)
                pe.wait_ge(S["sc_used"], v * TILES)
                mm(ps[0:AL, 6, 0:P], wdn_s[:, :], xcur[:, :], start=True, stop=True).then_inc(S["lat_full"], 1)

            def attention_qkv(v):
                pe.wait_ge(S["lat_ready"], v)
                mm(ps[:, 6, P:2 * P], xcur[:, :], wq_s[:, :], start=True, stop=True)
                mm(ps[:, 6, 2 * P:4 * P], lat[:, :], wup_s[:, :], start=True, stop=True).then_inc(S["a_full"], 1)

            def heads_to_features(v):
                pe.wait_ge(S["a_o"], v)
                pe.wait_ge(S["sc_used"], v * TILES + 2)
                tr(ps[:, 6, 0:P], on[:, :], ident).then_inc(S["ot_full"], 1)

            def attention_project(v):
                pe.wait_ge(S["gate0_read"], v)
                mm(ps[:, 7, 0:P], wout_s[:, :], oT[:, :], start=True, stop=True).then_inc(S["at_full"], 1)

            pe.wait_ge(S["casts"], 3)
            pe.wait_ge(S["pool_ready"], 3)

            def proj(v, l, t, n0=0, n1=4):
                if n0 == 0:
                    pe.wait_ge(S["wqk_loaded"], l * 16 + 16)
                    if t in (0, TILES):
                        pe.wait_ge(S["xsa_ready"], v + 1 + t // TILES)
                    wait(pe, S["qn_ready"], v * TILES + t)
                c = XPAD + (t % TILES) * P
                for n in range(n0, n1):
                    last = mm(ps[:, n, :], xsa[:, c:c + P], wqk[:, n * 512:(n + 1) * 512], start=True, stop=True)
                    if n % 2 == 1:
                        last.then_inc(S["qk_full"], 1)

            def window_tokens(v, i):
                bank, full = ring_take(v, ("xd", i))
                for j in range(XD_USE):
                    c = (XD_USE * i + j) * W
                    last = tr(bank[:, j * P:(j + 1) * P], xsa[:, c:c + P], ident)
                last.then_inc(full, 1)

            def to_features(v, t, i0, i1):
                r = rot[:, t % 2, :, :].rearrange("p h e -> p (h e)")
                for i in range(i0, i1):
                    if i % 2 == 0:
                        pe.wait_ge(S["rot_ready"], (v * TILES + t) * 2 + i // 2 + 1)
                    bank, full = ring_take(v, ("t", t, i))
                    for j in range(4):
                        c = 4 * i + j
                        last = tr(bank[:, j * P:(j + 1) * P], r[:, c * P:(c + 1) * P], ident)
                    last.then_inc(full, 1)

            def local_scores(v, t, prev, half, at=None):
                if half == 0:
                    wait(pe, S["sc_used"], v * TILES + t)
                    ring_emptied(pe, v, ("t", t, 2), ("t", t, 3))
                    if t == 0 and at is not None:
                        pe.wait_ge(S["a_bias"], v)
                    if t == 2 and at is not None:
                        pe.wait_ge(S["ot_ready"], v)
                    if t == 3 and at is not None:
                        pe.wait_ge(S["acc_done"], v)
                    if prev and t == 1:
                        pe.wait_ge(S["x1_ready"], v)
                    if prev and t == 3:
                        pe.wait_ge(S["x_done"], v + B)
                    mk = maskb[:, 1 if t == 0 else 0, :].unsqueeze(1).to_broadcast([P, PAIRS, 2 * W])
                    for e in range(2):
                        mm(ps[:, 6 + e, :], identb[:, :], mk, start=True, stop=False, skip_group_check=True)
                for p in range(half * PAIRS // 2, (half + 1) * PAIRS // 2):
                    for i in range(WT):
                        w = t * WT + i
                        for e in range(2):
                            last = mm(ps[W * i:W * i + W, 6 + e, p * 2 * W:(p + 1) * 2 * W],
                                      qT[64 * e:64 * e + 64, t % 2, p, W * i:W * i + W],
                                      kT[64 * e:64 * e + 64, p, W * w:W * w + 2 * W],
                                      start=False, stop=(p == PAIRS - 1), skip_group_check=True)
                if half == 1:
                    last.then_inc(S["sc_full"], 1)

            def probs_to_keys(v, t):
                pe.wait_ge(S["pn_ready"], v * TILES + t + 1)
                for i in range(2):
                    bank, full = ring_take(v, ("p", t, i))
                    for j in range(4):
                        last = tr(bank[:, j * P:(j + 1) * P], pn[:, 4 * i + j, :, :].rearrange("q e k -> q (e k)"), ident)
                    last.then_inc(full, 1)

            def weigh_tokens(v, t, k0=0, k1=4):
                if k0 == 0:
                    ring_emptied(pe, v, ("p", t, 0), ("p", t, 1))
                for k in range(k0, k1):
                    bank, full = ring_take(v, ("y", t, k))
                    wp, e = k // 2, k % 2
                    for i in range(2):
                        wi = 2 * wp + i
                        last = mm(bank[:, i * 256:(i + 1) * 256], xd[64 * e:64 * e + 64, (t % TILES) * WT + wi + 2 * (1 - e), :],
                                  pT[64 * e:64 * e + 64, :, W * wi:W * wi + W], start=True, stop=True)
                    last.then_inc(full, 1)

            def attention_out(v, l, e, p0=0, p1=PAIRS):
                if e == 0:
                    pe.wait_ge(S["m_ready"], l * 2 + 2)
                    ring_emptied(pe, v, ("y", -1, 2), ("y", -1, 3))
                    pe.wait_ge(S["sc_used"], UNITS * TILES if isinstance(v, int) and v == UNITS else v * TILES + 1)
                for p in range(p0, p1):
                    last = mm(ps[:, 7, :], mh[:, e, p, :], yT[:, e, p, :], start=(e + p == 0), stop=(e == 1 and p == PAIRS - 1))
                if e == 1 and p1 == PAIRS:
                    last.then_inc(S["attn_full"], 1)

            def to_tokens(v):
                pe.wait_ge(S["xsf_ready"], v)
                bank, full = ring_take(v, ("ln",))
                for t in range(TILES):
                    last = tr(bank[:, t * P:(t + 1) * P], xsf[:, t * P:(t + 1) * P], ident)
                last.then_inc(full, 1)

            def normed_to_features(v):
                pe.wait_ge(S["xn_ready"], v)
                bank, full = ring_take(v, ("xn",))
                for t in range(TILES):
                    last = tr(bank[:, t * P:(t + 1) * P], xn[:, t, :], ident)
                last.then_inc(full, 1)

            def widen(v, l, c):
                if c == 0:
                    pe.wait_ge(S["ffn_loaded"], l * 48 + 48)
                    ring_emptied(pe, v, ("xn",))
                m = P if c < FC - 1 else FREM
                for key, c0 in (("gate", F), ("val", 0)):
                    bank, full = ffn_take(v, key, c)
                    mm(bank[0:m, :], w1_s[:, c0 + c * P:c0 + c * P + m], xnT, start=True, stop=True).then_inc(full, 1)

            def narrow(v):
                if not (isinstance(v, int) and v == UNITS):
                    pe.wait_ge(S["sc_used"], v * TILES + 3)
                for c in range(FC):
                    m = P if c < FC - 1 else FREM
                    ffn_done(pe, v, "val", c)
                    last = mm(ps[:, 6, :], w2_s[0:m, c, :], hT[0:m, c, :], start=(c == 0), stop=(c == FC - 1))
                last.then_inc(S["out_full"], 1)

            def turn(v, l, b, prev, nxt, at):
                to_m = not (isinstance(b, int) and b == 0)
                if to_m:
                    pe.wait_ge(S["m_ready"], l * 2 + 1)
                proj(v, l, 1, 0, 2)
                to_features(v, 0, 0, 2)
                if to_m:
                    pe.wait_ge(S["m_ready"], l * 2 + 2)
                proj(v, l, 1, 2, 3)
                if at is not None:
                    latent(v)
                to_features(v, 0, 2, 4)
                if at is not None:
                    attention_qkv(v)
                proj(v, l, 1, 3, 4)
                local_scores(v, 0, prev, 0, at)
                if prev:
                    probs_to_keys(v, -1)
                local_scores(v, 0, prev, 1, at)
                if prev:
                    weigh_tokens(v, -1)
                for n in range(4):
                    window_tokens(v, n)
                    proj(v, l, 2, n, n + 1)
                window_tokens(v, 4)
                window_tokens(v, 5)
                if prev:
                    attention_out(v, prev[0], 0)
                to_features(v, 1, 0, 2)
                if prev:
                    attention_out(v, prev[0], 1, 0, 2)
                to_features(v, 1, 2, 3)
                if prev:
                    attention_out(v, prev[0], 1, 2, 4)
                if prev:
                    attention_out(v, prev[0], 1, 4, PAIRS)
                to_features(v, 1, 3, 4)
                probs_to_keys(v, 0)
                local_scores(v, 1, prev, 0)
                weigh_tokens(v, 0, 0, 2)
                local_scores(v, 1, prev, 1)
                if prev:
                    to_tokens(v)
                weigh_tokens(v, 0, 2, 4)
                proj(v, l, 3, 0, 2)
                to_features(v, 2, 0, 2)
                if at is not None:
                    heads_to_features(v)
                proj(v, l, 3, 2, 3)
                to_features(v, 2, 2, 4)
                proj(v, l, 3, 3, 4)
                local_scores(v, 2, prev, 0, at)
                probs_to_keys(v, 1)
                local_scores(v, 2, prev, 1, at)
                weigh_tokens(v, 1)
                if prev:
                    normed_to_features(v)
                if nxt:
                    proj(v, nxt[0], TILES, 0, 2)
                if prev:
                    widen(v, prev[0], 0)
                if nxt:
                    proj(v, nxt[0], TILES, 2, 4)
                if prev:
                    widen(v, prev[0], 1)
                to_features(v, 3, 0, 2)
                if prev:
                    widen(v, prev[0], 2)
                if at is not None:
                    attention_project(v)
                to_features(v, 3, 2, 4)
                if prev:
                    narrow(v)
                probs_to_keys(v, 2)
                local_scores(v, 3, prev, 0, at)
                weigh_tokens(v, 2, 0, 2)
                local_scores(v, 3, prev, 1, at)
                weigh_tokens(v, 2, 2, 4)

            def build_m(l):
                pe.wait_ge(S["mw_loaded"], l * 32 + 32)
                pe.wait_ge(S["qn_ready"], l * (B * TILES) + (TILES + 1))
                for e in range(2):
                    for p in range(PAIRS):
                        last = mm(ps[:, 2 * e + p // 4, (p % 4) * D:(p % 4 + 1) * D], wv_s[64 * e:64 * e + 64, p, :],
                                  wo_s[64 * e:64 * e + 64, p, :], start=True, stop=True)
                    last.then_inc(S["m_full"], 1)

            def after():
                probs_to_keys(UNITS, -1)
                weigh_tokens(UNITS, -1)
                attention_out(UNITS, L - 1, 0)
                attention_out(UNITS, L - 1, 1)
                to_tokens(UNITS)
                normed_to_features(UNITS)
                for c in range(FC):
                    widen(UNITS, L - 1, c)
                narrow(UNITS)

            proj(0, 0, 0)
            run_turns(pe, turn, build_m, after)
            pe.wait_ge(S["sum_ready"], 1)
            for b in range(B):
                for t in range(TILES):
                    last = tr(ps[:, b, t * P:(t + 1) * P], xT[:, b * T + t * P:b * T + (t + 1) * P], ident)
                last.then_inc(S["fin_full"], 1)

        @block.scalar
        def _(act):
            fn = nc.scalar.activation
            act.wait_ge(S["a_loaded"], 7 * 16)

            def take_tile(v):
                fn(xcur[:, :], accT[:, bass.ts(v - 1, P)], ACT.Copy).then_inc(S["xcur_ready"], 1)

            def latent(v):
                act.wait_ge(S["lat_full"], v)
                fn(lat[:, :], ps[0:AL, 6, 0:P], ACT.Identity, bias=avs[0:AL, A_BDOWN:A_BDOWN + 1]).then_inc(S["lat_ready"], 1)

            def attention_exp(v):
                act.wait_ge(S["a_sub"], v)
                fn(att[:, :, :], att[:, :, :], ACT.Exp, scale=float(AD) ** -0.5).then_inc(S["a_exp"], 1)

            def heads_to_features(v):
                act.wait_ge(S["ot_full"], v)
                fn(oT[:, :], ps[:, 6, 0:P], ACT.Copy).then_inc(S["ot_ready"], 1)

            act.wait_ge(S["pool_ready"], 3)

            def shift(dst, src, signal):
                fn(dst[0:64, :], src[0:64, :], ACT.Copy)
                fn(dst[64:P, 1:T], src[64:P, 0:T - 1], ACT.Copy).then_inc(signal, 1)

            def shift_input(v, b):
                act.wait_ge(S["x_done"], v + 1)
                wait(act, S["qk_full"], v * (TILES * 2))
                shift(xsa[:, XPAD:XPAD + T], xT[:, bass.ts(b, T)], S["xsa_ready"])

            def squares(v, t, s):
                act.wait_ge(S["qk_full"], (v * TILES + t) * 2 + s + 1)
                fn(sq[:, s * H:(s + 1) * H, :].rearrange("p h e -> p (h e)"), ps[:, 2 * s:2 * s + 2, :],
                   ACT.Square).then_inc(S["sq_ready"], 1)

            def window_tokens(v, i):
                bank, free = ring_read(act, v, ("xd", i))
                fn(xd[:, XD_USE * i:XD_USE * (i + 1), :].rearrange("p w d -> p (w d)"), bank[:, 0:XD_USE * P], ACT.Copy).then_inc(free, 1)

            def features(v, t, *quarters):
                for i in quarters:
                    bank, free = ring_read(act, v, ("t", t, i))
                    src = bank.rearrange("p (j q) -> p j q", q=P)
                    p0 = i % 2 * 4
                    dst = qT[:, t % 2, p0:p0 + 4, :] if i < 2 else kT[:, p0:p0 + 4, W + t * P:W + (t + 1) * P]
                    fn(dst, src, ACT.Copy).then_inc(free, 1)

            def exps(v, t):
                act.wait_ge(S["sc_used"], v * TILES + t + 1)
                fn(sm[:, :, :], sm[:, :, :], ACT.Exp).then_inc(S["p_ready"], 1)

            def probs(v, t):
                for i in range(2):
                    bank, free = ring_read(act, v, ("p", t, i))
                    fn(pT[:, 4 * i:4 * i + 4, :], bank.rearrange("p (j q) -> p j q", q=P), ACT.Copy).then_inc(free, 1)

            def weighed(v, t, *quarters):
                for i in quarters or range(4):
                    bank, free = ring_read(act, v, ("y", t, i))
                    c0 = (t % TILES) * P + i // 2 * 2 * W
                    fn(yT[:, i % 2, :, c0:c0 + 2 * W].rearrange("f p (i q) -> f i p q", q=W),
                       bank.rearrange("f (i p q) -> f i p q", p=PAIRS, q=W), ACT.Copy).then_inc(free, 1)

            def shift_middle(v):
                act.wait_ge(S["x1_ready"], v)
                shift(xsf[:, :], x1[:, :], S["xsf_ready"])

            def tokens(v):
                bank, free = ring_read(act, v, ("ln",))
                fn(xn[:, :, :].rearrange("p t d -> p (t d)"), bank, ACT.Copy).then_inc(free, 1)

            def normed(v, l):
                act.wait_ge(S["ffn_loaded"], l * 48 + 48)
                bank, free = ring_read(act, v, ("xn",))
                fn(xnT, bank, ACT.Identity, scale=fv[:, V_G:V_G + 1], bias=fv[:, V_B:V_B + 1]).then_inc(free, 1)

            def gates(v, c):
                m = P if c < FC - 1 else FREM
                bank, free = ffn_read(act, v, "gate", c)
                fn(gl[0:m, c, :], bank[0:m, :], ACT.Gelu, bias=fv[0:m, V_GATE + c:V_GATE + c + 1]).then_inc(free, 1)

            def turn(v, l, b, prev, nxt, at):
                if at is not None:
                    take_tile(v)
                features(v, 0, 0, 1)
                if prev:
                    exps(v, -1)
                if at is not None:
                    latent(v)
                features(v, 0, 2, 3)
                squares(v, 1, 0)
                squares(v, 1, 1)
                if prev:
                    probs(v, -1)
                    weighed(v, -1)
                window_tokens(v, 0)
                window_tokens(v, 1)
                window_tokens(v, 2)
                squares(v, 2, 0)
                window_tokens(v, 3)
                window_tokens(v, 4)
                window_tokens(v, 5)
                squares(v, 2, 1)
                exps(v, 0)
                if at is not None:
                    attention_exp(v)
                features(v, 1, 0, 1, 2, 3)
                probs(v, 0)
                if prev:
                    shift_middle(v)
                weighed(v, 0, 0, 1)
                if prev:
                    tokens(v)
                weighed(v, 0, 2, 3)
                exps(v, 1)
                features(v, 2, 0, 1)
                squares(v, 3, 0)
                if at is not None:
                    heads_to_features(v)
                features(v, 2, 2, 3)
                squares(v, 3, 1)
                if nxt:
                    shift_input(v + 1, nxt[1])
                probs(v, 1)
                weighed(v, 1)
                if prev:
                    normed(v, prev[0])
                exps(v, 2)
                if nxt:
                    squares(v, TILES, 0)
                if prev:
                    gates(v, 0)
                if nxt:
                    squares(v, TILES, 1)
                if prev:
                    gates(v, 1)
                features(v, 3, 0, 1)
                if prev:
                    gates(v, 2)
                features(v, 3, 2, 3)
                probs(v, 2)
                weighed(v, 2)

            def copy_m(l):
                for e in range(2):
                    act.wait_ge(S["m_full"], l * 2 + e + 1)
                    fn(mh[:, e, :, :].rearrange("c p f -> c (p f)"), ps[:, 2 * e:2 * e + 2, :], ACT.Copy).then_inc(S["m_ready"], 1)

            def after():
                exps(UNITS, -1)
                probs(UNITS, -1)
                weighed(UNITS, -1)
                shift_middle(UNITS)
                tokens(UNITS)
                normed(UNITS, L - 1)
                for c in range(FC):
                    gates(UNITS, c)

            shift_input(0, 0)
            squares(0, 0, 0)
            squares(0, 0, 1)
            run_turns(act, turn, copy_m, after)

        @block.vector
        def _(dve):
            v = nc.vector

            class Steps:
                def __init__(self, sem_, base):
                    self.sem, self.base, self.n = sem_, base, 0

                def done(self, ins):
                    self.n += 1
                    ins.then_inc(self.sem, 1)
                    dve.wait_ge(self.sem, self.base + self.n)

            def rsqrt(step, src, c0, c1):
                y, t = ny[:, c0:c1], nt[:, c0:c1]
                step.done(v.tensor_scalar(t.bitcast(I32), src.bitcast(I32), 1, None, ALU.logical_shift_right))
                step.done(v.tensor_scalar(y.bitcast(I32), t.bitcast(I32), -1.0, float(RSQRT_MAGIC), ALU.mult, ALU.add))
                for _ in range(3):
                    step.done(v.scalar_tensor_tensor(out=t, in0=y, scalar=-0.5, in1=y, op0=ALU.mult, op1=ALU.mult))
                    step.done(v.tensor_tensor(t, t, src, ALU.mult))
                    step.done(v.scalar_tensor_tensor(out=y, in0=t, scalar=1.5, in1=y, op0=ALU.add, op1=ALU.mult))

            def token_stats(step, source, n, variances):
                for i in range(n):
                    last = v.bn_stats(st6[:, i, :], source(i))
                step.done(last)
                v.memset(spare[:, 0:1], 0.0)
                for i in range(n):
                    last = v.bn_aggr(mv[:, i, :], st6[:, i, :])
                step.done(last)
                step.done(v.tensor_scalar(variances, mv[:, 0:n, 1], EPS, None, ALU.add))

            dve.wait_ge(S["x_loaded"], 16)
            step = Steps(S["pro_chain"], 0)
            token_stats(step, lambda i: xtok[:, i, :], B * TILES, ss0[:, :])
            rsqrt(step, ss0[:, :], 0, B * TILES)
            for i in range(B * TILES):
                ins = v.tensor_scalar(xn0[:, i, :], xtok[:, i, :], mv[:, i, 0:1], ny[:, i:i + 1], ALU.subtract, ALU.mult)
                if i % TILES == TILES - 1:
                    ins.then_inc(S["xn0_ready"], 1)
            dve.wait_ge(S["const_loaded"], 16)
            v.tensor_copy(identb[:, :], ident).then_inc(S["casts"], 1)
            v.tensor_copy(maskb[:, 0, :], consts[:, C_MASK:C_MASK + 2 * W]).then_inc(S["casts"], 1)
            v.tensor_copy(maskb[:, 1, :], consts[:, C_MASK0:C_MASK0 + 2 * W]).then_inc(S["casts"], 1)
            for b in range(B):
                dve.wait_ge(S["pro_full"], b + 1)
                v.tensor_copy(accT[:, b * T:(b + 1) * T], ps[:, b, :])
                v.tensor_copy(xT[:, b * T:(b + 1) * T], ps[:, b, :]).then_inc(S["x_done"], 1)

            dve.wait_ge(S["a_loaded"], 7 * 16)
            def attention_rotate(v, tile):
                step = Steps(S["a_chain"], (v - 1) * A_STEPS)
                dve.wait_ge(S["a_full"], v)
                nc.vector.tensor_tensor(qkv[:, :], ps[:, 6, P:4 * P], abb[:, :], ALU.add).then_inc(S["a_bias"], 1)
                dve.wait_ge(S["a_bias"], v)
                def heads(a):
                    return a[:, 0:2 * P].rearrange("p (h d) -> p h d", d=AD)
                def table(i, o, n):
                    return atb[:, i, bass.ds(tile, 1), o:o + n].to_broadcast([P, 2 * AH, n])
                nc.vector.tensor_tensor(heads(rqk), heads(qkv), table(0, 0, AD), ALU.mult)
                n = AD // 2
                for o, i in ((0, n), (n, 0)):
                    last = nc.vector.tensor_tensor(heads(rsin)[:, :, o:o + n], heads(qkv)[:, :, i:i + n], table(1, o, n), ALU.mult)
                step.done(last)
                nc.vector.tensor_tensor(rqk[:, :], rqk[:, :], rsin[:, :], ALU.add).then_inc(S["a_rot"], 1)

            def attention_scores(v):
                step = Steps(S["a_chain"], (v - 1) * A_STEPS + 1)
                dve.wait_ge(S["a_qk"], v)
                step.done(nc.vector.tensor_reduce(att[:, :, :].rearrange("p h g -> p (h g)"),
                                                  prod[:, :].rearrange("p (n d) -> p n d", d=AD), AXX, ALU.add))
                step.done(nc.vector.tensor_reduce(am[:, 0, :], att[:, :, :], AXX, ALU.max, negate=True))
                nc.vector.tensor_tensor(att[:, :, :], att[:, :, :], am[:, 0, :].unsqueeze(2).to_broadcast([P, AH, AH]),
                                        ALU.add).then_inc(S["a_sub"], 1)

            def attention_weigh(v):
                step = Steps(S["a_chain"], (v - 1) * A_STEPS + 3)
                dve.wait_ge(S["a_exp"], v)
                step.done(nc.vector.tensor_reduce(am[:, 1, :], att[:, :, :], AXX, ALU.add))
                nc.vector.reciprocal(am[:, 2, :], am[:, 1, :])
                dve.wait_ge(S["a_pv"], v)
                step.done(nc.vector.tensor_reduce(oraw[:, :], prod[:, :].rearrange("p (n g) -> p n g", g=AH), AXX, ALU.add))
                nc.vector.tensor_tensor(on[:, :].rearrange("p (h d) -> p h d", d=AD), oraw[:, :].rearrange("p (h d) -> p h d", d=AD),
                                        am[:, 2, :].unsqueeze(2).to_broadcast([P, AH, AD]), ALU.mult).then_inc(S["a_o"], 1)

            def attention_store(v):
                dve.wait_ge(S["at_full"], v)
                nc.vector.tensor_scalar(accT[:, bass.ts(v - 1, P)], ps[:, 7, 0:P], avs[:, A_BOUT:A_BOUT + 1], None,
                                        ALU.add).then_inc(S["acc_done"], 1)

            def squared_norms(v, t):
                for s in range(2):
                    dve.wait_ge(S["sq_ready"], (v * TILES + t) * 2 + s + 1)
                    last = nc.vector.tensor_reduce(ss[:, s * H:(s + 1) * H], sq[:, s * H:(s + 1) * H, :], AXX, ALU.add)
                last.then_inc(S["norm_chain"], 1)

            def norms(v, t):
                step = Steps(S["norm_chain"], (v * TILES + t) * TILE_STEPS + 1)
                dve.wait_ge(S["norm_chain"], (v * TILES + t) * TILE_STEPS + 1)
                step.done(nc.vector.tensor_scalar(ss[:, 0:2 * H], ss[:, 0:2 * H], 1e-24, None, ALU.max))
                rsqrt(step, ss[:, 0:2 * H], 0, 2 * H)
                assert step.n == TILE_STEPS - 1

            def normalised(v, t):
                wait(dve, S["rotc_done"], (v * TILES + t) * 2)
                for s in range(2):
                    last = nc.vector.tensor_tensor(qn[:, s * H:(s + 1) * H, :],
                                            ps[:, 2 * s:2 * s + 2, :].rearrange("p k (h e) -> p (k h) e", e=E),
                                            ny[:, s * H:(s + 1) * H].unsqueeze(2).to_broadcast([P, H, E]), ALU.mult)
                last.then_inc(S["qn_ready"], 1)

            def add_sines(v, t, s):
                n, heads = (v * TILES + t) * 2 + s + 1, slice(s * H, (s + 1) * H)
                dve.wait_ge(S["ms_ready"], n)
                dve.wait_ge(S["rotc_done"], n)
                nc.vector.tensor_tensor(rot[:, t % 2, heads, :], rot[:, t % 2, heads, :], ms[:, heads, :], ALU.add).then_inc(S["rot_ready"], 1)

            def normalise_squared(v, t):
                norms(v, t)
                normalised(v, t)

            def normalise(v, t):
                squared_norms(v, t)
                normalise_squared(v, t)

            def sine_terms(v, l, t):
                dve.wait_ge(S["qn_ready"], v * TILES + t + 1)
                dve.wait_ge(S["tab_ready"], l * 4 + 4)
                wait(dve, S["rot_ready"], (v * TILES + t) * 2)
                for s in range(2):
                    for half in range(2):
                        o, i = half * E // 2, (1 - half) * E // 2
                        last = nc.vector.tensor_tensor(ms[:, s * H:(s + 1) * H, o:o + E // 2],
                                                qn[:, s * H:(s + 1) * H, i:i + E // 2],
                                                tab[:, 2 * s + 1, t % TILES, o:o + E // 2].unsqueeze(1).to_broadcast([P, H, E // 2]), ALU.mult)
                    last.then_inc(S["ms_ready"], 1)

            def shift_scores(v, t):
                step = Steps(S["soft_chain"], (v * TILES + t) * SOFT_STEPS)
                wait(dve, S["sc_used"], v * TILES + t)
                dve.wait_ge(S["sc_full"], v * TILES + t + 1)
                sc = ps[:, 6:8, :].rearrange("p e (h k) -> p (e h) k", k=2 * W)
                step.done(nc.vector.tensor_reduce(negm[:, :], sc, AXX, ALU.max, negate=True))
                wait(dve, S["pn_ready"], v * TILES + t)
                nc.vector.tensor_tensor(sm[:, :, :], sc, negm[:, :].unsqueeze(2).to_broadcast([P, H, 2 * W]),
                                 ALU.add).then_inc(S["sc_used"], 1)

            def sum_probs(v, t):
                step = Steps(S["soft_chain"], (v * TILES + t) * SOFT_STEPS + 1)
                wait(dve, S["rinv_ready"], v * TILES + t)
                dve.wait_ge(S["p_ready"], v * TILES + t + 1)
                step.done(nc.vector.tensor_reduce(psum_[:, :], sm[:, :, :], AXX, ALU.add))
                nc.vector.reciprocal(rinv[:, t % 2, :], psum_[:, :]).then_inc(S["rinv_ready"], 1)

            def middle(v, b):
                dve.wait_ge(S["attn_full"], v)
                dve.wait_ge(S["x_done"], v - 1 + B)
                nc.vector.tensor_tensor(x1[:, :], ps[:, 7, :], xT[:, bass.ts(b, T)], ALU.add).then_inc(S["x1_ready"], 1)

            def stats(v):
                step = Steps(S["ln_chain"], (v - 1) * LN_STEPS)
                ring_emptied(dve, v, ("ln",))
                token_stats(step, lambda i: xn[:, i, :], TILES, ss[:, 2 * H:2 * H + TILES])

            def norm_tokens(v):
                step = Steps(S["ln_chain"], (v - 1) * LN_STEPS + 3)
                rsqrt(step, ss[:, 2 * H:2 * H + TILES], 2 * H, 2 * H + TILES)
                for i in range(TILES):
                    last = nc.vector.tensor_scalar(xn[:, i, :], xn[:, i, :], mv[:, i, 0:1], ny[:, 2 * H + i:2 * H + i + 1], ALU.subtract, ALU.mult)
                last.then_inc(S["xn_ready"], 1)

            def gated(v, c):
                m = P if c < FC - 1 else FREM
                ffn_done(dve, v, "gate", c)
                bank, free = ffn_read(dve, v, "val", c)
                nc.vector.scalar_tensor_tensor(out=hT[0:m, c, :], in0=bank[0:m, :], scalar=fv[0:m, V_A + c:V_A + c + 1],
                                        in1=gl[0:m, c, :], op0=ALU.add, op1=ALU.mult).then_inc(free, 1)

            def finish(v, b):
                dve.wait_ge(S["out_full"], v)
                dve.wait_ge(S["x1_ready"], v)
                nc.vector.scalar_tensor_tensor(out=xT[:, bass.ts(b, T)], in0=ps[:, 6, :], scalar=fv[:, V_B2:V_B2 + 1], in1=x1[:, :],
                                        op0=ALU.add, op1=ALU.add).then_inc(S["x_done"], 1)

            def turn(v, l, b, prev, nxt, at):
                if at is not None:
                    attention_rotate(v, at)
                normalise(v, 1)
                shift_scores(v, 0)
                if at is not None:
                    attention_scores(v)
                sine_terms(v, l, 1)
                add_sines(v, 1, 0)
                sum_probs(v, 0)
                add_sines(v, 1, 1)
                normalise(v, 2)
                sine_terms(v, l, 2)
                if prev:
                    middle(v, prev[1])
                if at is not None:
                    attention_weigh(v)
                add_sines(v, 2, 0)
                add_sines(v, 2, 1)
                shift_scores(v, 1)
                if prev:
                    stats(v)
                sum_probs(v, 1)
                if prev:
                    norm_tokens(v)
                normalise(v, 3)
                shift_scores(v, 2)
                sine_terms(v, l, 3)
                if prev:
                    gated(v, 0)
                add_sines(v, 3, 0)
                if prev:
                    gated(v, 1)
                sum_probs(v, 2)
                add_sines(v, 3, 1)
                if prev:
                    gated(v, 2)
                if nxt:
                    squared_norms(v, TILES)
                if at is not None:
                    attention_store(v)
                if prev:
                    finish(v, prev[1])
                if nxt:
                    normalise_squared(v, TILES)
                    sine_terms(v, nxt[0], TILES)
                    add_sines(v, TILES, 0)
                shift_scores(v, 3)
                if nxt:
                    add_sines(v, TILES, 1)
                sum_probs(v, 3)

            def after():
                middle(UNITS, B - 1)
                stats(UNITS)
                norm_tokens(UNITS)
                for c in range(FC):
                    gated(UNITS, c)
                finish(UNITS, B - 1)

            normalise(0, 0)
            sine_terms(0, 0, 0)
            add_sines(0, 0, 0)
            add_sines(0, 0, 1)
            run_turns(dve, turn, lambda l: None, after)

            dve.wait_ge(S["x_done"], B + L * B)
            dve.wait_ge(S["acc_done"], B * TILES)
            v.tensor_tensor(xT[:, :], xT[:, :], accT[:, :], ALU.add).then_inc(S["sum_ready"], 1)
            for b in range(B):
                dve.wait_ge(S["fin_full"], b + 1)
                dve.wait_ge(S["x_loaded"], 32)
                tok = ytok[:, b * TILES:(b + 1) * TILES, :].rearrange("p n d -> p (n d)")
                v.tensor_tensor(tok, ps[:, b, :], tok, ALU.add).then_inc(S["y_ready"], 1)

        @block.gpsimd
        def _(pool):
            g = nc.gpsimd
            pool.wait_ge(S["x_done"], B)
            g.memset(xsa[:, :], 0.0).then_inc(S["pool_ready"], 1)
            pool.wait_ge(S["pool_ready"], 1)
            g.memset(xsf[:, :], 0.0).then_inc(S["pool_ready"], 1)
            pool.wait_ge(S["pool_ready"], 2)
            g.memset(kT[:, :, 0:W], 0.0).then_inc(S["pool_ready"], 1)
            pool.wait_ge(S["pool_ready"], 3)
            pool.wait_ge(S["tabb_loaded"], 16)

            def attention_products(v):
                pool.wait_ge(S["a_rot"], v)
                q = rqk[:, 0:P].rearrange("p (h d) -> p h d", d=AD).unsqueeze(2).to_broadcast([P, AH, AH, AD])
                k = rqk[:, P:2 * P].rearrange("p (g d) -> p g d", d=AD).unsqueeze(1).to_broadcast([P, AH, AH, AD])
                g.tensor_tensor(prod[:, :].rearrange("p (h g d) -> p h g d", g=AH, d=AD), q, k, ALU.mult).then_inc(S["a_qk"], 1)

            def attention_values(v):
                pool.wait_ge(S["a_exp"], v)
                probs = att[:, :, :].unsqueeze(2).to_broadcast([P, AH, AD, AH])
                values = qkv[:, 2 * P:3 * P].rearrange("p (d g) -> p d g", g=AH).unsqueeze(1).to_broadcast([P, AH, AD, AH])
                g.tensor_tensor(prod[:, :].rearrange("p (h d g) -> p h d g", d=AD, g=AH), probs, values, ALU.mult).then_inc(S["a_pv"], 1)

            def tables(l):
                pool.wait_ge(S["qkv_loaded"], l * 16 + 16)
                wait(pool, S["ms_ready"], l * (B * TILES * 2))
                wait(pool, S["rotc_done"], l * (B * TILES * 2))
                for k in range(4):
                    g.tensor_tensor(tab[:, k, :, :], tabb[:, k, :, :], qkvec[:, k, :].unsqueeze(1).to_broadcast([P, TILES, E]),
                                    ALU.mult).then_inc(S["tab_ready"], 1)

            def rotate(v, l, t):
                pool.wait_ge(S["tab_ready"], l * 4 + 4)
                pool.wait_ge(S["qn_ready"], v * TILES + t + 1)
                for s in range(2):
                    heads = slice(s * H, (s + 1) * H)
                    g.tensor_tensor(rot[:, t % 2, heads, :], qn[:, heads, :],
                                    tab[:, 2 * s, t % TILES, :].unsqueeze(1).to_broadcast([P, H, E]), ALU.mult).then_inc(S["rotc_done"], 1)

            def divide(v, t, prev):
                pool.wait_ge(S["rinv_ready"], v * TILES + t + 1)
                if t or prev:
                    ring_emptied(pool, v, ("p", t - 1, 1))
                g.tensor_tensor(pn[:, :, :, :].rearrange("q p e k -> q e p k"),
                                sm[:, :, :].rearrange("q (e p) k -> q e p k", e=2),
                                rinv[:, t % 2, :].rearrange("q (e p) -> q e p", e=2).unsqueeze(3)
                                .to_broadcast([P, 2, PAIRS, 2 * W]), ALU.mult).then_inc(S["pn_ready"], 1)

            def turn(v, l, b, prev, nxt, at):
                for t in range(TILES):
                    if t == 0 and at is not None:
                        attention_products(v)
                    if t < TILES - 1:
                        rotate(v, l, t + 1)
                    elif nxt:
                        if isinstance(b, int) and b == B - 1:
                            tables(nxt[0])
                        rotate(v, nxt[0], TILES)
                    if t == 0 and at is not None:
                        attention_values(v)
                    divide(v, t, prev)

            tables(0)
            rotate(0, 0, 0)
            run_turns(pool, turn, lambda l: None, lambda: None)


def constants():
    import numpy as np
    f = np.float32
    cst = np.zeros((P, C_END), f)
    cst[:, C_ID:C_ID + P] = np.eye(P)
    i, j = np.arange(P)[:, None] % W, np.arange(2 * W)[None]
    seen = (i <= j) & (j <= i + W)
    cst[:, C_MASK:C_MASK + 2 * W] = np.where(seen, 0, NEG)
    cst[:, C_MASK0:C_MASK0 + 2 * W] = np.where(seen & ((np.arange(P)[:, None] >= W) | (j >= W)), 0, NEG)
    t = np.arange(T, dtype=f)
    inv = (f(1) / f(10000) ** (np.arange(0, AD, 2, dtype=f) / f(AD))).astype(f)
    fr = t[:, None] * inv[None]
    c, s = np.cos(fr), np.sin(fr)
    tiled = lambda a: a.reshape(TILES, P, -1).transpose(1, 0, 2)
    atab = np.stack([tiled(np.concatenate(a, 1)) for a in ((c, c), (-s, s))], 1).astype(f)
    half = np.arange(0, E, 2, dtype=f)
    inv = (f(1) / f(10000) ** (half / f(E))).astype(f)
    fr = t[:, None] * inv[None]
    base = ((half + f(0.4 * E)) / f(1.4 * E)).astype(f)
    sc = base[None] ** ((t - T // 2) / f(W // 2))[:, None]
    c, s = np.cos(fr), np.sin(fr)
    both = lambda a, b: np.concatenate([a, b], 1)
    tabs = [both(8 * c * sc, 8 * c * sc), both(-8 * s * sc, 8 * s * sc), both(c / sc, c / sc), both(-s / sc, s / sc)]
    ftab = np.stack([tiled(a) for a in tabs], 1).astype(f)
    return cst, atab, ftab


def kernel(**inputs):
    import numpy as np
    import concourse.bacc as bacc
    from concourse.bass_utils import run_bass_kernel_spmd

    a = {k[3:]: np.asarray(v) for k, v in inputs.items()}
    swap64 = (np.arange(E) + E // 2) % E

    def column(*vs):
        return np.stack([np.concatenate([v, np.zeros(P - len(v), v.dtype)]) for v in vs], 1)

    wup, bup = (a[k].reshape(-1, AH, 2, AD) for k in ("attn_Wup", "attn_bup"))
    wup, bup = (np.concatenate([z[:, :, 0].reshape(-1, P), z[:, :, 1].transpose(0, 2, 1).reshape(-1, P)], 1) for z in (wup, bup))
    w2 = np.zeros((L, FC * P, D), a["ffn_W2"].dtype)
    w2[:, 0:F] = a["ffn_W2"]
    cuts = lambda v: [v[i:i + P] for i in range(0, F, P)]
    qs, ks = a["ffn_q_scale"], a["ffn_k_scale"]
    cst, atab, ftab = constants()
    arrays = {
        "x": a["attn_x"],
        "avec": column(a["attn_bout"], a["attn_bdown"]),
        "abias": np.concatenate([a["attn_bq"], bup[0]]),
        "wq": a["attn_Wq"],
        "wdown": a["attn_Wdown"],
        "wup": wup,
        "wout": a["attn_Wout"],
        "wqkv": a["ffn_Wqkv"],
        "wvt": a["ffn_Wqkv"][:, :, 2 * INNER:].transpose(0, 2, 1),
        "wo": a["ffn_Wo"],
        "w1": a["ffn_W1"],
        "w2": w2,
        "fvec": np.stack([column(a["ffn_ln_g"][i], a["ffn_ln_b"][i], *cuts(a["ffn_b1"][i, 0:F]), *cuts(a["ffn_b1"][i, F:]),
                                 a["ffn_b2"][i]) for i in range(L)]),
        "qks": np.stack([qs, qs[:, swap64], ks, ks[:, swap64]], 1),
        "cst": cst, "atab": atab, "ftab": ftab,
    }
    nc = bacc.Bacc("TRN2", target_bir_lowering=False, num_devices=1)
    arrays = {f"in_{k}": np.ascontiguousarray(v) for k, v in arrays.items()}
    args = [nc.dram_tensor(k, v.shape, mybir.dt.from_np(v.dtype), kind="ExternalInput").ap() for k, v in arrays.items()]
    y = nc.dram_tensor("out_0", (B, T, D), F32, kind="ExternalOutput").ap()
    program(nc, *args, y)
    r = run_bass_kernel_spmd(nc, [arrays], core_ids=[0])
    return r.results[0]["out_0"]
```
